# Optimizing a Trainium2 kernel written in Bass

```python
import numpy as np
import jax
import jax.numpy as jnp

def _softmax(x, axis=-1):
    return jax.nn.softmax(x, axis=axis)

def _gelu(x):
    return jax.nn.gelu(x, approximate=True)

def _silu(x):
    return jax.nn.silu(x)

def _sigmoid(x):
    return jax.nn.sigmoid(x)

def _layernorm(x, axis=-1, eps=1e-05):
    m = jnp.mean(x, axis=axis, keepdims=True)
    v = jnp.var(x, axis=axis, keepdims=True)
    return (x - m) / jnp.sqrt(v + eps)

def _scatter_add(tgt, idx, src, axis=0):
    return tgt.at[idx].add(src)

def _segment_sum(src, seg, n):
    return jax.ops.segment_sum(src, seg, n)
kernel_name = 'mk_macaron_d1_jaxref_r8_a3ce60'

def setup_inputs(seed: int=0):
    np.random.seed(seed)
    _w = jnp.asarray

    def _L0_attn_setup():
        import jax, jax.numpy as jnp
        import numpy as np
        import math
        D_MODEL = 512
        N_HEADS = 32
        HEAD_DIM = D_MODEL // N_HEADS
        CLIP_QKV = 8.0
        ALIBI_BIAS_MAX = 8
        LN_EPS = 1e-05

        def _alibi_slopes(total_num_heads: int, alibi_bias_max: int) -> jnp.ndarray:
            next_p2 = 2 ** math.ceil(math.log2(total_num_heads))
            m = jnp.arange(1, next_p2 + 1, dtype=jnp.float32) * (alibi_bias_max / next_p2)
            slopes = 1.0 / jnp.power(2.0, m)
            if next_p2 != total_num_heads:
                slopes = jnp.concatenate([slopes[1::2], slopes[::2]])[:total_num_heads]
            return slopes

        def _layer_norm(x, w, b):
            mu = jnp.mean(x, axis=-1, keepdims=True)
            var = jnp.var(x, axis=-1, keepdims=True)
            return (x - mu) * jax.lax.rsqrt(var + LN_EPS) * w + b
        key = jax.random.key(seed)
        k0, k1, k2 = jax.random.split(key, 3)
        B, S = (2, 256)
        return {'hidden_states': jax.random.normal(k0, (B, S, D_MODEL), dtype=jnp.float32), 'w_qkv': jax.random.normal(k1, (3 * D_MODEL, D_MODEL), dtype=jnp.float32) * 0.02, 'q_ln_w': jnp.ones((D_MODEL,), jnp.float32), 'q_ln_b': jnp.zeros((D_MODEL,), jnp.float32), 'k_ln_w': jnp.ones((D_MODEL,), jnp.float32), 'k_ln_b': jnp.zeros((D_MODEL,), jnp.float32), 'w_out': jax.random.normal(k2, (D_MODEL, D_MODEL), dtype=jnp.float32) * 0.02}
    _L0_attn_in = _L0_attn_setup()

    def _L0_ffn_setup():
        import jax, jax.numpy as jnp
        import numpy as np
        RMS_EPS = 1e-05
        key = jax.random.key(seed)
        k1, k2, k3, k4 = jax.random.split(key, 4)
        B, S, H, I = (1, 256, 512, 1792)
        x = jax.random.normal(k1, (B, S, H), dtype=jnp.float32)
        ln_w = jnp.ones((H,), dtype=jnp.float32)
        gate_w = jax.random.normal(k2, (I, H), dtype=jnp.float32) * 0.02
        up_w = jax.random.normal(k3, (I, H), dtype=jnp.float32) * 0.02
        down_w = jax.random.normal(k4, (H, I), dtype=jnp.float32) * 0.02
        return {'x': x, 'ln_w': ln_w, 'gate_w': gate_w, 'up_w': up_w, 'down_w': down_w}
    _L0_ffn_in = _L0_ffn_setup()
    _d = {'L0_attn_hidden_states': _L0_attn_in['hidden_states'], 'L0_attn_w_qkv': _L0_attn_in['w_qkv'], 'L0_attn_q_ln_w': _L0_attn_in['q_ln_w'], 'L0_attn_q_ln_b': _L0_attn_in['q_ln_b'], 'L0_attn_k_ln_w': _L0_attn_in['k_ln_w'], 'L0_attn_k_ln_b': _L0_attn_in['k_ln_b'], 'L0_attn_w_out': _L0_attn_in['w_out'], 'L0_ffn_ln_w': _L0_ffn_in['ln_w'], 'L0_ffn_gate_w': _L0_ffn_in['gate_w'], 'L0_ffn_up_w': _L0_ffn_in['up_w'], 'L0_ffn_down_w': _L0_ffn_in['down_w']}
    _x0 = _d['L0_attn_hidden_states']
    _d['L0_attn_hidden_states'] = jax.random.normal(jax.random.fold_in(jax.random.key(seed), 1), (2, 512, 512), dtype=_x0.dtype)
    del _x0
    return _d

def reference(L0_attn_hidden_states, L0_attn_w_qkv, L0_attn_q_ln_w, L0_attn_q_ln_b, L0_attn_k_ln_w, L0_attn_k_ln_b, L0_attn_w_out, L0_ffn_ln_w, L0_ffn_gate_w, L0_ffn_up_w, L0_ffn_down_w):

    def _L0_attn_ref(hidden_states, w_qkv, q_ln_w, q_ln_b, k_ln_w, k_ln_b, w_out):
        import jax, jax.numpy as jnp
        import numpy as np
        import math
        D_MODEL = 512
        N_HEADS = 32
        HEAD_DIM = D_MODEL // N_HEADS
        CLIP_QKV = 8.0
        ALIBI_BIAS_MAX = 8
        LN_EPS = 1e-05

        def _alibi_slopes(total_num_heads: int, alibi_bias_max: int) -> jnp.ndarray:
            next_p2 = 2 ** math.ceil(math.log2(total_num_heads))
            m = jnp.arange(1, next_p2 + 1, dtype=jnp.float32) * (alibi_bias_max / next_p2)
            slopes = 1.0 / jnp.power(2.0, m)
            if next_p2 != total_num_heads:
                slopes = jnp.concatenate([slopes[1::2], slopes[::2]])[:total_num_heads]
            return slopes

        def _layer_norm(x, w, b):
            mu = jnp.mean(x, axis=-1, keepdims=True)
            var = jnp.var(x, axis=-1, keepdims=True)
            return (x - mu) * jax.lax.rsqrt(var + LN_EPS) * w + b
        B, S, D = hidden_states.shape
        qkv = jnp.einsum('bsd,ed->bse', hidden_states, w_qkv)
        qkv = jnp.clip(qkv, -CLIP_QKV, CLIP_QKV)
        q, k, v = jnp.split(qkv, 3, axis=-1)
        q = _layer_norm(q, q_ln_w, q_ln_b)
        k = _layer_norm(k, k_ln_w, k_ln_b)
        q = q.reshape(B, S, N_HEADS, HEAD_DIM)
        k = k.reshape(B, S, N_HEADS, HEAD_DIM)
        v = v.reshape(B, S, N_HEADS, HEAD_DIM)
        scale = HEAD_DIM ** (-0.5)
        scores = jnp.einsum('bqhd,bkhd->bhqk', q, k) * scale
        pos = jnp.arange(S)
        rel = pos[None, :] - pos[:, None]
        slopes = _alibi_slopes(N_HEADS, ALIBI_BIAS_MAX)
        bias = slopes[:, None, None] * rel.astype(jnp.float32)
        causal = rel <= 0
        scores = jnp.where(causal[None, None], scores + bias[None], -jnp.inf)
        probs = jax.nn.softmax(scores, axis=-1)
        attn = jnp.einsum('bhqk,bkhd->bqhd', probs, v).reshape(B, S, D)
        return jnp.einsum('bsd,ed->bse', attn, w_out)

    def _L0_ffn_ref(x, ln_w, gate_w, up_w, down_w):
        import jax, jax.numpy as jnp
        import numpy as np
        RMS_EPS = 1e-05
        var = jnp.mean(jnp.square(x), axis=-1, keepdims=True)
        nx = x * jax.lax.rsqrt(var + RMS_EPS) * ln_w
        g = jnp.einsum('bsh,ih->bsi', nx, gate_w)
        u = jnp.einsum('bsh,ih->bsi', nx, up_w)
        return jnp.einsum('bsi,hi->bsh', jax.nn.silu(g) * u, down_w)
    x = L0_attn_hidden_states
    x = x + 0.5 * _L0_ffn_ref(_layernorm(x, axis=-1), L0_ffn_ln_w, L0_ffn_gate_w, L0_ffn_up_w, L0_ffn_down_w)
    x = x + _L0_attn_ref(_layernorm(x, axis=-1), L0_attn_w_qkv, L0_attn_q_ln_w, L0_attn_q_ln_b, L0_attn_k_ln_w, L0_attn_k_ln_b, L0_attn_w_out)
    x = x + 0.5 * _L0_ffn_ref(_layernorm(x, axis=-1), L0_ffn_ln_w, L0_ffn_gate_w, L0_ffn_up_w, L0_ffn_down_w)
    return x

_drawn_inputs = setup_inputs


def setup_inputs(seed=0):
    import zlib

    import numpy as np

    out = dict(_drawn_inputs(seed))
    spreads = {'L0_attn_q_ln_w': (1.0, 0.6),
     'L0_attn_q_ln_b': (0.0, 0.8),
     'L0_attn_k_ln_w': (1.0, 0.6),
     'L0_attn_k_ln_b': (0.0, 0.8),
     'L0_ffn_ln_w': (1.0, 0.2)}
    factors = {}
    for name, (base, spread) in spreads.items():
        noise = np.random.default_rng([zlib.crc32(name.encode()), seed]).standard_normal(out[name].shape)
        drawn = base * np.exp(spread * noise) if base else spread * noise
        out[name] = jnp.asarray(drawn.astype(out[name].dtype))
    for name, factor in factors.items():
        out[name] = (out[name] * factor).astype(out[name].dtype)
    return out
```

```python
from contextlib import ExitStack

import numpy as np

import concourse.bass as bass
from concourse import mybir

ALU = mybir.AluOpType
ACT = mybir.ActivationFunctionType
AX = mybir.AxisListType
F32 = mybir.dt.float32
F32R = mybir.dt.float32r
BF16 = mybir.dt.bfloat16

P = 128
B, S, D = 2, 512, 512
I = 1792
H = 32
HD = D // H
KC = D // P
TILES = B * S // P
NCH = I // P
FIRST = 7
SLOTS = FIRST + 1
HALVES = B * S // 512
UNITS = NCH * HALVES
EPS = 1e-5
CLIP = 8.0
MASKED = -3.0e38

RAW = 3
PIECE = KC * 2 * P

GH = 4
GROUPS = H // GH
NG = B * GROUPS
QT = S // P
ROWS = 64
CON = 6
A_UNITS = 12
B_OPS = 6
VW = HD + 1


def ffn_pieces(f):
    def gu(c):
        return ("gu", f, c)

    def wd(c):
        return ("wd", f, c)

    after = {-1: [gu(0), gu(1), wd(0)]}
    for c in range(5):
        after[c] = [gu(c + 2), wd(c + 1)]
    after[5] = [gu(7), wd(6)]
    after[6] = [gu(8)]
    after[7] = [gu(9)]
    after[8] = [gu(10), wd(7), wd(8)]
    after[9] = [gu(11), wd(9)]
    after[10] = [gu(12), wd(10)]
    after[11] = [gu(13), wd(11)]
    after[12] = [wd(12), wd(13)]
    after[13] = []
    return after


def fills_at(s, i):
    out = []
    if i == 0:
        out = [("O", 0, s - 3)]
    elif i == 1:
        out = [("QB", 0, s - 1)]
    elif i == 2:
        out = [("QB", 1, s - 1)]
    elif i == 3:
        out = [("K", 0, s + 1)]
    elif i == 4:
        out = [("K", 1, s + 1)]
    elif i == 5:
        out = [("QA", 0, s + 1), ("QA", 1, s + 1)]
    return [f for f in out if 0 <= f[2] < NG]


def outproj_at(s):
    for b in range(B):
        t = s - ((b + 1) * GROUPS + 3)
        if 0 <= t < QT:
            return b, t
    return None


STEPS = range(-1, NG + 3 + QT)


def number_attention():
    fills, units = {}, {}
    for s in STEPS:
        for i in range(B_OPS):
            for n in (2 * i, 2 * i + 1):
                if 0 <= s < NG and n < A_UNITS:
                    units[("A", s, n)] = len(units)
            for f in fills_at(s, i):
                fills[f] = len(fills)
        if outproj_at(s):
            fills[("AT",) + outproj_at(s)] = len(fills)
            units[("Y",) + outproj_at(s)] = len(units)
    return fills, units


def a_unit(n):
    if n < 4:
        return n // 2, [n % 2, n % 2 + 2]
    return 2 + (n - 4) // GH, [(n - 4) % GH]


def b_op(n):
    if n < 4:
        kc, first = n // 2, 2 * (n % 2)
        return kc, [(first, 0, 0), (first + 1, 1, 0)]
    kc = n - 2
    return kc, [(hh, hh % 2, (S - kc * P) * (hh // 2)) for hh in (0, 2, 1, 3)]


def build(nc, x_in, w_gu, w_down, w_qkv, w_out, ln_w, q_w, q_b, k_w, k_b, con_q, con_k, out):
    persistent = ExitStack()
    with persistent:
        def sem(name):
            return persistent.enter_context(nc.semaphore(name))

        def allocate(stack, name, shape, dt):
            return stack.enter_context(nc.sbuf_tensor(name, shape, dt))

        def sb(name, shape, dt=F32):
            return allocate(persistent, name, shape, dt)

        x = sb("x", [P, TILES, D])
        raw = sb("raw", [P, RAW, PIECE])
        lnw_row = sb("lnw_row", [P, D])
        ident = sb("ident", [P, P])
        ident_bf = sb("ident_bf", [P, P], BF16)
        mask_a = sb("mask_a", [P, P], BF16)
        mask_b = sb("mask_b", [P, P], BF16)
        y = sb("y", [P, 2, D])
        junk = sb("junk", [P, D], BF16)
        stats = sb("stats", [P, 2, 6])
        mean_var = sb("mean_var", [P, 2, 2])
        power = sb("power", [P, 1])
        rstd = sb("rstd", [P, 2, 1])
        sumsq = sb("sumsq", [P, 2, 1])
        rms = sb("rms", [P, 2, 1])
        q_stats = sb("q_stats", [P, 2, 6])
        q_mean_var = sb("q_mean_var", [P, 4, 2])
        q_rstd = sb("q_rstd", [P, 4, 1])
        neg_max = sb("neg_max", [P, 2, QT, GH])
        rsum = sb("rsum", [P, QT, GH])

        far = ExitStack()
        xt_hi = far.enter_context(nc.sbuf_tensor("xt_hi", [P, KC, B * S], F32R, side="right"))
        xt_lo = far.enter_context(nc.sbuf_tensor("xt_lo", [P, KC, B * S], F32R, side="right"))

        with ExitStack() as ffn_stage:
            gu_hi = allocate(ffn_stage, "gu_hi", [P, 2, 2, KC, P], F32R)
            gu_lo = allocate(ffn_stage, "gu_lo", [P, 2, 2, KC, P], F32R)
            wd_hi = allocate(ffn_stage, "wd_hi", [P, FIRST, D], F32R)
            wd_lo = allocate(ffn_stage, "wd_lo", [P, FIRST, D], F32R)
            act_hi = allocate(ffn_stage, "act_hi", [P, SLOTS, B * S], F32R)
            act_lo = allocate(ffn_stage, "act_lo", [P, SLOTS, B * S], F32R)
            silu_g = allocate(ffn_stage, "silu_g", [P, 2, 512], F32)
            act_f = allocate(ffn_stage, "act_f", [P, 2, 512], F32)

        mid = ExitStack()
        qn = allocate(mid, "qn", [P, B, QT, D], F32)
        kn = allocate(mid, "kn", [P, B, QT, D], F32)
        vext = allocate(mid, "vext", [P, B, QT, H, VW], F32)
        wo_hi = allocate(mid, "wo_hi", [P, KC, D], F32R)
        wo_lo = allocate(mid, "wo_lo", [P, KC, D], F32R)
        cq = allocate(mid, "cq", [P, QT, H, CON], F32)
        ck = allocate(mid, "ck", [P, QT, H, CON], F32)
        with ExitStack() as qkv_stage:
            qkv_hi = allocate(qkv_stage, "qkv_hi", [P, KC, 3 * D], F32R)
            qkv_lo = allocate(qkv_stage, "qkv_lo", [P, KC, 3 * D], F32R)
            qc = allocate(qkv_stage, "qc", [P, 4, D], F32)
            wb = allocate(qkv_stage, "wb", [P, 4, D], F32)
        far.close()

        with ExitStack() as att:
            stack_k = allocate(att, "stack_k", [P, 2, QT, GH, ROWS], F32R)
            stack_q = allocate(att, "stack_q", [P, 3, QT, GH, ROWS], F32R)
            k_t = allocate(att, "k_t", [P, 4, 2, S], F32R)
            qa_t = allocate(att, "qa_t", [P, 2, 2, S], F32R)
            qb_t = allocate(att, "qb_t", [P, 2, 2, S], F32R)
            probs = allocate(att, "probs", [P, 3, 1024], F32)
            o_t = allocate(att, "o_t", [P, 2, S], F32)
            attn = allocate(att, "attn", [P, 2, QT, D], F32)
            at_hi = allocate(att, "at_hi", [P, 2, KC, P], F32R)
            at_lo = allocate(att, "at_lo", [P, 2, KC, P], F32R)
        mid.close()

        ps = persistent.enter_context(nc.psum_tensor("ps", [P, 8, 512], F32))
        PV, TB = 6, 7

        x_loaded = [sem(f"x_loaded{t}") for t in range(TILES)]
        rows_loaded = sem("rows_loaded")
        cons_loaded = sem("cons_loaded")
        raw_loaded = [sem(f"raw_loaded{n}") for n in range(RAW)]
        piece_hi = sem("piece_hi")
        piece_lo = sem("piece_lo")
        ident_ready = sem("ident_ready")
        masks_ready = sem("masks_ready")
        dve_step = sem("dve_step")
        pool_step = sem("pool_step")
        var_ready = sem("var_ready")
        rstd_ready = sem("rstd_ready")
        y_ready = sem("y_ready")
        sq_ready = sem("sq_ready")
        rms_ready = sem("rms_ready")
        norm_ready = sem("norm_ready")
        norm_turned = sem("norm_turned")
        xt_hi_ready = sem("xt_hi_ready")
        xt_ready = sem("xt_ready")
        gate_done = sem("gate_done")
        up_done = sem("up_done")
        silu_done = sem("silu_done")
        act_f_ready = sem("act_f_ready")
        act_hi_ready = sem("act_hi_ready")
        act_ready = sem("act_ready")
        down_done = sem("down_done")
        x_updated = sem("x_updated")
        qkv_done = sem("qkv_done")
        qkv_clipped = sem("qkv_clipped")
        q_var_ready = sem("q_var_ready")
        q_rstd_ready = sem("q_rstd_ready")
        q_normed = sem("q_normed")
        qk_ready = sem("qk_ready")
        wb_ready = sem("wb_ready")
        vones_ready = sem("vones_ready")
        stack_ready = sem("stack_ready")
        pv_cleared = sem("pv_cleared")
        t_filled = sem("t_filled")
        t_emptied = sem("t_emptied")
        a_filled = sem("a_filled")
        a_emptied = sem("a_emptied")
        shift_ready = sem("shift_ready")
        b_filled = sem("b_filled")
        exp_done = sem("exp_done")
        pv_step = sem("pv_step")
        o_t_ready = sem("o_t_ready")
        at_hi_ready = sem("at_hi_ready")
        stored = sem("stored")

        pieces = []
        for f in range(2):
            after = ffn_pieces(f)
            pieces += [p for c in range(-1, NCH) for p in after[c]]
            if f == 0:
                pieces += [("qkv", 0, j) for j in range(6)] + [("wo", 0, j) for j in range(2)]
        piece_no = {p: n for n, p in enumerate(pieces)}
        fill_no, unit_no = number_attention()
        unit_at = {n: unit for unit, n in unit_no.items()}
        FFN_UPDATES = 2 * TILES
        ATT_UPDATES = TILES

        def updates_before(f):
            return f * (FFN_UPDATES + ATT_UPDATES)

        def piece_source(p):
            kind, _, c = p
            if kind == "gu":
                return w_gu[c], PIECE
            if kind == "wd":
                return w_down[c], D
            return (w_qkv if kind == "qkv" else w_out)[c], PIECE

        def piece_views(p):
            kind, _, c = p
            slot = raw[:, piece_no[p] % RAW, :]
            if kind == "gu":
                v = slot.rearrange("p (a k n) -> p a k n", a=2, k=KC)
                return v, gu_hi[:, c % 2], gu_lo[:, c % 2]
            if kind == "wd":
                return slot[:, 0:D], wd_hi[:, c % FIRST, :], wd_lo[:, c % FIRST, :]
            v = slot.rearrange("p (k n) -> p k n", k=KC)
            hi, lo = (qkv_hi, qkv_lo) if kind == "qkv" else (wo_hi, wo_lo)
            return v, hi[:, :, 256 * c:256 * c + 256], lo[:, :, 256 * c:256 * c + 256]

        block = persistent.enter_context(nc.Block())

        @block.sync
        def _(sp):
            for t in range(TILES):
                sp.dma_start(x[:, t, :], x_in[t * P:(t + 1) * P, :]).then_inc(x_loaded[t], 16)
                if t == 1:
                    sp.dma_start(lnw_row[:, :], ln_w.broadcast_to([P, D])).then_inc(rows_loaded, 16)
                if t < RAW:
                    source, n = piece_source(pieces[t])
                    sp.dma_start(raw[:, t, 0:n], source).then_inc(raw_loaded[t], 16)
            for n, p in enumerate(pieces):
                if n < RAW:
                    continue
                sp.wait_ge(piece_lo, n - RAW + 1)
                source, size = piece_source(p)
                sp.dma_start(raw[:, n % RAW, 0:size], source).then_inc(raw_loaded[n % RAW], 16)
                if p == ("qkv", 0, RAW):
                    sp.dma_start(cq[:, :, :, :], con_q).then_inc(cons_loaded, 16)
                    sp.dma_start(ck[:, :, :, :], con_k).then_inc(cons_loaded, 16)
                    for j, row in enumerate((q_w, q_b, k_w, k_b)):
                        sp.dma_start(wb[:, j, :], row.broadcast_to([P, D])).then_inc(cons_loaded, 16)
            base = updates_before(1) + TILES
            for t in range(TILES):
                sp.wait_ge(x_updated, base + t + 1)
                sp.dma_start(out[t * P:(t + 1) * P, :], x[:, t, :]).then_inc(stored, 16)
            sp.wait_ge(stored, 16 * TILES)

        @block.gpsimd
        def _(pool):
            steps = [0]

            def link(ins):
                steps[0] += 1
                ins.then_inc(pool_step, 1)
                pool.wait_ge(pool_step, steps[0])

            link(nc.gpsimd.memset(ident[:, :], 0.0))
            link(nc.gpsimd.affine_select(out=ident[:, :], in_=ident[:, :], compare_op=ALU.not_equal, fill=1.0,
                                         base=0, pattern=[[-1, P]], channel_multiplier=1))
            nc.gpsimd.memset(power[:, :], -0.5).then_inc(ident_ready, 1)
            pool.wait_ge(ident_ready, 1)

            nc.gpsimd.tensor_copy(ident_bf[:, :], ident[:, :]).then_inc(masks_ready, 1)
            link(nc.gpsimd.memset(mask_a[:, :], 0.0))
            link(nc.gpsimd.memset(mask_b[:, :], 0.0))
            nc.gpsimd.affine_select(out=mask_a[:, :], in_=mask_a[:, :], compare_op=ALU.is_ge, fill=MASKED, base=0,
                                    pattern=[[-1, P]], channel_multiplier=1).then_inc(masks_ready, 1)
            nc.gpsimd.affine_select(out=mask_b[:, :], in_=mask_b[:, :], compare_op=ALU.is_ge, fill=MASKED, base=0,
                                    pattern=[[1, P]], channel_multiplier=-1).then_inc(masks_ready, 1)

            def inverse_root(dst, src, scale):
                link(nc.gpsimd.tensor_scalar(dst, src, scale, EPS, ALU.mult, ALU.add))
                return nc.gpsimd.tensor_tensor(dst, dst, power[:, :], ALU.pow)

            def norm_tile(phase, t):
                n = phase * TILES + t
                pool.wait_ge(var_ready, n + 1)
                inverse_root(rstd[:, n % 2, :], mean_var[:, n % 2, 1:2], 1.0).then_inc(rstd_ready, 1)
                if phase != 1:
                    m = (phase // 2) * TILES + t
                    pool.wait_ge(sq_ready, m + 1)
                    inverse_root(rms[:, n % 2, :], sumsq[:, n % 2, :], 1.0 / D).then_inc(rms_ready, 1)

            def split_low(p):
                v, hi, lo = piece_views(p)
                pool.wait_ge(piece_hi, piece_no[p] + 1)
                nc.gpsimd.tensor_tensor(lo, v, hi.bitcast(F32), ALU.subtract).then_inc(piece_lo, 1)

            def ffn(f):
                after = ffn_pieces(f)
                for t in range(TILES):
                    norm_tile(2 * f, t)
                    if t == 3:
                        for p in after[-1]:
                            split_low(p)
                for c in range(NCH):
                    for b in range(HALVES):
                        u = UNITS * f + 2 * c + b
                        pool.wait_ge(act_hi_ready, u + 1)
                        at = slice(512 * b, 512 * b + 512)
                        nc.gpsimd.tensor_tensor(act_lo[:, c % SLOTS, at], act_f[:, u % 2, :],
                                                act_hi[:, c % SLOTS, at].bitcast(F32),
                                                ALU.subtract).then_inc(act_ready, 1)
                    for p in after[c]:
                        split_low(p)

            ffn(0)
            for t in range(TILES):
                norm_tile(1, t)
            for j in range(6):
                split_low(("qkv", 0, j))
            pool.wait_ge(cons_loaded, 16 * 6)
            link(nc.gpsimd.tensor_scalar(wb[:, 0:2, :], wb[:, 0:2, :], float(HD) ** -0.5, None, ALU.mult))
            for j in range(2):
                split_low(("wo", 0, j))
            for t in range(TILES):
                for j in range(2):
                    n = 2 * t + j
                    pool.wait_ge(q_var_ready, n + 1)
                    inverse_root(q_rstd[:, n % 4, :], q_mean_var[:, n % 4, 1:2], 1.0).then_inc(q_rstd_ready, 1)
                for j in range(2):
                    n = 2 * t + j
                    dst = (qn, kn)[j][:, t // QT, t % QT, :]
                    pool.wait_ge(q_normed, n + 1)
                    link(nc.gpsimd.tensor_tensor(dst, qc[:, n % 4, :], wb[:, 2 * j, :], ALU.mult))
                    nc.gpsimd.tensor_tensor(dst, dst, wb[:, 2 * j + 1, :], ALU.add).then_inc(qk_ready, 1)

            pool.wait_ge(qkv_clipped, 3 * TILES)
            pool.wait_ge(qk_ready, 2 * TILES)
            link(nc.gpsimd.memset(stack_k[:, :, :, :, :].bitcast(F32), 0.0))
            link(nc.gpsimd.memset(stack_q[:, :, :, :, :].bitcast(F32), 0.0))

            def stack_group(G):
                b, g = G // GROUPS, G % GROUPS
                sk, sq = stack_k[:, G % 2], stack_q[:, G % 3]
                heads = slice(GH * g, GH * g + GH)
                q = qn[:, b].rearrange("p t (h d) -> p t h d", d=HD)[:, :, heads, :]
                k = kn[:, b].rearrange("p t (h d) -> p t h d", d=HD)[:, :, heads, :]
                if G >= 2:
                    pool.wait_ge(t_filled, fill_no["K", 1, G - 2] + 1)
                nc.gpsimd.tensor_copy(sk[:, :, :, 16:32], k)
                nc.gpsimd.tensor_copy(sk[:, :, :, 0:CON], ck[:, :, heads, :])
                link(nc.gpsimd.tensor_copy(sk[:, :, :, 32:48], k))
                nc.gpsimd.tensor_tensor(sk[:, :, :, 48:64], k, sk[:, :, :, 32:48].bitcast(F32), ALU.subtract)
                if G >= 3:
                    pool.wait_ge(t_filled, fill_no["QB", 1, G - 3] + 1)
                nc.gpsimd.tensor_copy(sq[:, :, :, 16:32], q)
                nc.gpsimd.tensor_copy(sq[:, :, :, 0:CON], cq[:, :, heads, :])
                link(nc.gpsimd.tensor_copy(sq[:, :, :, 48:64], q))
                nc.gpsimd.tensor_tensor(sq[:, :, :, 32:48], q, sq[:, :, :, 48:64].bitcast(F32),
                                        ALU.subtract).then_inc(stack_ready, 1)

            for G in range(NG):
                stack_group(G)
            ffn(1)

        @block.scalar
        def _(act):
            def turn_high(phase, t):
                n = phase * TILES + t
                act.wait_ge(norm_turned, n + 1)
                nc.scalar.activation(xt_hi[:, :, t * P:(t + 1) * P],
                                     ps[:, 6 + n % 2, :].rearrange("p (k n) -> p k n", k=KC),
                                     ACT.Copy).then_inc(xt_hi_ready, 1)

            def square(phase, t):
                n = phase * TILES + t
                act.wait_ge(y_ready, (phase // 2) * TILES + t + 1)
                nc.scalar.activation(junk[:, :], y[:, n % 2, :], ACT.Square,
                                     accum_out=sumsq[:, n % 2, :]).then_inc(sq_ready, 1)

            def ffn_norms(phase):
                for t in range(TILES + 1):
                    if t < TILES:
                        square(phase, t)
                    if t >= 1:
                        turn_high(phase, t - 1)

            def high(u):
                c, b = (u % UNITS) // 2, u % 2
                act.wait_ge(act_f_ready, u + 1)
                if c >= SLOTS:
                    act.wait_ge(down_done, FFN_UPDATES * (u // UNITS) + TILES)
                nc.scalar.activation(act_hi[:, c % SLOTS, 512 * b:512 * b + 512], act_f[:, u % 2, :],
                                     ACT.Copy).then_inc(act_hi_ready, 1)

            def ffn(f):
                for u in range(UNITS * f, UNITS * f + UNITS):
                    act.wait_ge(gate_done, u + 1)
                    if u >= 2:
                        act.wait_ge(act_f_ready, u - 1)
                    nc.scalar.activation(silu_g[:, u % 2, :], ps[:, u % 2, :], ACT.Silu).then_inc(silu_done, 1)
                    if u > UNITS * f:
                        high(u - 1)
                high(UNITS * f + UNITS - 1)

            ffn_norms(0)
            ffn(0)
            for t in range(TILES):
                turn_high(1, t)

            def exp(G, n):
                idx = B_OPS * G + n
                kc, heads = b_op(n)
                bank = 2 + 2 * (idx % 2)
                act.wait_ge(b_filled, idx + 1)
                if idx >= 3:
                    act.wait_ge(pv_step, idx - 2)
                width = (S - kc * P) * len(heads) // 2
                nc.scalar.activation(probs[:, idx % 3, 0:2 * width].rearrange("p (a n) -> p a n", a=2),
                                     ps[:, bank:bank + 2, 0:width], ACT.Exp).then_inc(exp_done, 1)

            def evacuate(kind, j, G):
                n = fill_no[kind, j, G]
                dst = {"K": k_t[:, G % 4], "QA": qa_t[:, G % 2], "QB": qb_t[:, G % 2]}[kind][:, j, :]
                act.wait_ge(t_filled, n + 1)
                nc.scalar.activation(dst, ps[:, TB, :], ACT.Copy).then_inc(t_emptied, 1)

            act.wait_ge(qk_ready, 2 * TILES)
            act.wait_ge(qkv_clipped, 3 * TILES)
            for s in STEPS:
                for i in range(B_OPS):
                    if 0 <= s - 2 < NG:
                        exp(s - 2, i)
                    for kind, j, G in fills_at(s, i):
                        if kind in ("QA", "QB") or (kind == "K" and j == 0):
                            evacuate(kind, j, G)
                if 0 <= s - 2 < NG:
                    G = s - 2
                    act.wait_ge(pv_step, B_OPS * G + B_OPS)
                    if G >= 2:
                        act.wait_ge(t_filled, fill_no["O", 0, G - 2] + 1)
                    nc.scalar.activation(o_t[:, G % 2, :], ps[:, PV, :], ACT.Copy).then_inc(o_t_ready, 1)
                if outproj_at(s):
                    b, t = outproj_at(s)
                    m = b * QT + t
                    act.wait_ge(t_filled, fill_no["AT", b, t] + 1)
                    if m >= 2:
                        act.wait_ge(a_filled, unit_no["Y", (m - 2) // QT, (m - 2) % QT] + 1)
                    nc.scalar.activation(at_hi[:, m % 2], ps[:, TB, :].rearrange("p (k n) -> p k n", k=KC),
                                         ACT.Copy).then_inc(at_hi_ready, 1)
            ffn_norms(2)
            ffn(1)

        @block.vector
        def _(dve):
            steps = [0]

            def link(ins):
                steps[0] += 1
                ins.then_inc(dve_step, 1)
                dve.wait_ge(dve_step, steps[0])

            def norm_stats(phase, t):
                n = phase * TILES + t
                if phase == 0:
                    dve.wait_ge(x_loaded[t], 16)
                else:
                    dve.wait_ge(x_updated, (FFN_UPDATES if phase == 1 else updates_before(1)) - TILES + t + 1)
                if n >= 2:
                    dve.wait_ge(rstd_ready, n - 1)
                link(nc.vector.bn_stats(stats[:, n % 2, :], x[:, t, :]))
                nc.vector.bn_aggr(mean_var[:, n % 2, :], stats[:, n % 2, :]).then_inc(var_ready, 1)

            def norm_apply(phase, t):
                n = phase * TILES + t
                dve.wait_ge(rstd_ready, n + 1)
                dve.wait_ge(var_ready, n + 1)
                if n >= 2:
                    dve.wait_ge(norm_turned, n - 1)
                nc.vector.tensor_scalar(y[:, n % 2, :], x[:, t, :], mean_var[:, n % 2, 0:1], rstd[:, n % 2, :],
                                        ALU.subtract, ALU.mult).then_inc(norm_ready if phase == 1 else y_ready, 1)

            def norm_rms(phase, t):
                n = phase * TILES + t
                dve.wait_ge(rms_ready, (phase // 2) * TILES + t + 1)
                if phase == 0 and t == 0:
                    dve.wait_ge(rows_loaded, 16)
                nc.vector.scalar_tensor_tensor(out=y[:, n % 2, :], in0=y[:, n % 2, :], scalar=rms[:, n % 2, :],
                                               in1=lnw_row[:, :], op0=ALU.mult, op1=ALU.mult).then_inc(norm_ready, 1)

            def turn_low(phase, t):
                n = phase * TILES + t
                at = slice(t * P, (t + 1) * P)
                dve.wait_ge(xt_hi_ready, n + 1)
                nc.vector.tensor_tensor(xt_lo[:, :, at], ps[:, 6 + n % 2, :].rearrange("p (k n) -> p k n", k=KC),
                                        xt_hi[:, :, at].bitcast(F32), ALU.subtract).then_inc(xt_ready, 1)

            def split_high(p):
                kind, f, c = p
                n = piece_no[p]
                v, hi, _ = piece_views(p)
                dve.wait_ge(raw_loaded[n % RAW], 16 * (n // RAW + 1))
                if kind == "gu" and c >= 2:
                    dve.wait_ge(up_done, UNITS * f + 2 * (c - 2) + 2)
                if kind == "wd" and c >= FIRST:
                    dve.wait_ge(down_done, FFN_UPDATES * f + TILES)
                nc.vector.tensor_copy(hi, v).then_inc(piece_hi, 1)

            def norms(phase, pieces_at=()):
                last = 2 if phase == 1 else 3
                for t in range(TILES + last):
                    if t < TILES:
                        norm_stats(phase, t)
                    if 1 <= t <= TILES:
                        norm_apply(phase, t - 1)
                    if phase != 1 and 2 <= t < TILES + 2:
                        norm_rms(phase, t - 2)
                    if t >= last:
                        turn_low(phase, t - last)
                    if t == 4:
                        for p in pieces_at:
                            split_high(p)

            def x_update(n, bank, scale):
                t = n % TILES
                if n >= TILES:
                    dve.wait_ge(x_updated, n - TILES + 1)
                nc.vector.scalar_tensor_tensor(out=x[:, t, :], in0=ps[:, bank, :], scalar=scale, in1=x[:, t, :],
                                               op0=ALU.mult, op1=ALU.add).then_inc(x_updated, 1)

            def ffn(f):
                after = ffn_pieces(f)
                base = updates_before(f)

                def round_out(r):
                    for t in range(TILES):
                        dve.wait_ge(down_done, FFN_UPDATES * f + TILES * r + t + 1)
                        x_update(base + TILES * r + t, 4 + t % 2, 0.5)

                for c in range(NCH):
                    if c == SLOTS:
                        round_out(0)
                    for b in range(HALVES):
                        u = UNITS * f + 2 * c + b
                        dve.wait_ge(silu_done, u + 1)
                        dve.wait_ge(up_done, u + 1)
                        if u >= 2:
                            dve.wait_ge(act_ready, u - 1)
                        nc.vector.tensor_tensor(act_f[:, u % 2, :], ps[:, 2 + u % 2, :], silu_g[:, u % 2, :],
                                                ALU.mult).then_inc(act_f_ready, 1)
                    for p in after[c]:
                        split_high(p)
                round_out(1)

            norms(0, ffn_pieces(0)[-1])
            ffn(0)
            norms(1)
            dve.wait_ge(x_updated, FFN_UPDATES)
            for j in range(6):
                split_high(("qkv", 0, j))
            nc.vector.memset(vext[:, :, :, :, HD:VW], 1.0).then_inc(vones_ready, 1)
            for j in range(2):
                split_high(("wo", 0, j))
            for t in range(TILES):
                for j in range(3):
                    n = 2 * t + j
                    bank = 3 * (t % 2) + j
                    dve.wait_ge(qkv_done, 3 * t + j + 1)
                    if j == 2:
                        nc.vector.tensor_scalar(vext[:, t // QT, t % QT, :, 0:HD],
                                                ps[:, bank, :].rearrange("p (h d) -> p h d", d=HD),
                                                CLIP, -CLIP, ALU.min, ALU.max).then_inc(qkv_clipped, 1)
                        continue
                    if n >= 4:
                        dve.wait_ge(qk_ready, n - 3)
                    nc.vector.tensor_scalar(qc[:, n % 4, :], ps[:, bank, :], CLIP, -CLIP,
                                            ALU.min, ALU.max).then_inc(qkv_clipped, 1)
                    dve.wait_ge(qkv_clipped, 3 * t + j + 1)
                    link(nc.vector.bn_stats(q_stats[:, j, :], qc[:, n % 4, :]))
                    nc.vector.bn_aggr(q_mean_var[:, n % 4, :], q_stats[:, j, :]).then_inc(q_var_ready, 1)
                for j in range(2):
                    n = 2 * t + j
                    dve.wait_ge(q_rstd_ready, n + 1)
                    dve.wait_ge(q_var_ready, n + 1)
                    nc.vector.tensor_scalar(qc[:, n % 4, :], qc[:, n % 4, :], q_mean_var[:, n % 4, 0:1],
                                            q_rstd[:, n % 4, :], ALU.subtract, ALU.mult).then_inc(q_normed, 1)

            dve.wait_ge(qk_ready, 2 * TILES)
            nc.vector.memset(ps[:, PV, :], 0.0).then_inc(pv_cleared, 1)

            def row_max(G, n):
                m = unit_no["A", G, n]
                qt, heads = a_unit(n)
                width = P * (qt + 1)
                dve.wait_ge(a_filled, m + 1)
                scores = ps[:, m % 2, 0:width * len(heads)].rearrange("p (h n) -> p h n", n=width)
                nc.vector.tensor_reduce(neg_max[:, G % 2, qt, heads[0]:heads[-1] + 1:2], scores,
                                        AX.X, ALU.max, negate=True).then_inc(a_emptied, 1)

            def shift(G):
                sq = stack_q[:, G % 3]
                m = neg_max[:, G % 2]
                dve.wait_ge(a_emptied, A_UNITS * (G + 1))
                dve.wait_ge(t_filled, fill_no["QA", 1, G] + 1)
                link(nc.vector.tensor_copy(sq[:, :, :, 4], m))
                nc.vector.tensor_tensor(sq[:, :, :, 5], m, sq[:, :, :, 4].bitcast(F32),
                                        ALU.subtract).then_inc(shift_ready, 1)

            for s in STEPS:
                for i in range(B_OPS):
                    for n in (2 * i, 2 * i + 1):
                        if 0 <= s < NG and n < A_UNITS:
                            row_max(s, n)
                    for kind, j, G in fills_at(s, i):
                        if kind == "K" and j == 1:
                            dve.wait_ge(t_filled, fill_no[kind, j, G] + 1)
                            nc.vector.tensor_copy(k_t[:, G % 4, j, :], ps[:, TB, :]).then_inc(t_emptied, 1)
                        if kind == "O":
                            b, g = G // GROUPS, G % GROUPS
                            dve.wait_ge(t_filled, fill_no[kind, j, G] + 1)
                            turned = ps[:, TB, :].rearrange("p (t h d) -> p t h d", t=QT, h=GH)
                            link(nc.vector.reciprocal(rsum[:, :, :], turned[:, :, :, HD]))
                            dst = attn[:, b].rearrange("p t (h d) -> p t h d", d=HD)[:, :, GH * g:GH * g + GH, :]
                            for qt in range(QT):
                                o = nc.vector.tensor_tensor(
                                    dst[:, qt], turned[:, qt, :, 0:HD],
                                    rsum[:, qt, :].unsqueeze(2).broadcast_to([P, GH, HD]), ALU.mult)
                            o.then_inc(t_emptied, 1)
                if 0 <= s < NG:
                    shift(s)
                if outproj_at(s):
                    b, t = outproj_at(s)
                    m = b * QT + t
                    dve.wait_ge(at_hi_ready, m + 1)
                    nc.vector.tensor_tensor(at_lo[:, m % 2], ps[:, TB, :].rearrange("p (k n) -> p k n", k=KC),
                                            at_hi[:, m % 2].bitcast(F32), ALU.subtract).then_inc(t_emptied, 1)
                    u = unit_no["Y", b, t]
                    dve.wait_ge(a_filled, u + 1)
                    x_update(FFN_UPDATES + m, u % 2, 1.0)
            dve.wait_ge(x_updated, updates_before(1))
            norms(2, ffn_pieces(1)[-1])
            ffn(1)

        @block.tensor
        def _(pe):
            def product(dst, w, v, first, last):
                nc.tensor.matmul(dst, w[0], v[0], start=first, stop=False)
                nc.tensor.matmul(dst, w[1], v[0], start=False, stop=False)
                return nc.tensor.matmul(dst, w[0], v[1], start=False, stop=last)

            def turn(phase, t):
                n = phase * TILES + t
                pe.wait_ge(norm_ready, n + 1)
                if n >= 2:
                    pe.wait_ge(xt_ready, n - 1)
                for k in range(KC):
                    last = nc.tensor.transpose(ps[:, 6 + n % 2, k * P:(k + 1) * P],
                                               y[:, n % 2, k * P:(k + 1) * P], ident[:, :])
                last.then_inc(norm_turned, 1)

            def unit(f, c, b):
                u = UNITS * f + 2 * c + b
                slot = c % 2
                pe.wait_ge(piece_lo, piece_no["gu", f, c] + 1)
                pe.wait_ge(xt_ready, 2 * TILES * f + 4 * (b + 1))
                if u >= 2:
                    pe.wait_ge(act_f_ready, u - 1)
                at = slice(512 * b, 512 * b + 512)
                for a, bank, done in ((0, u % 2, gate_done), (1, 2 + u % 2, up_done)):
                    for k in range(KC):
                        last = product(ps[:, bank, :], (gu_hi[:, slot, a, k, :], gu_lo[:, slot, a, k, :]),
                                       (xt_hi[:, k, at], xt_lo[:, k, at]), k == 0, k == KC - 1)
                    last.then_inc(done, 1)

            def down(f, r):
                chunks = range(FIRST * r, FIRST * r + FIRST)
                base = updates_before(f) + TILES * r
                pe.wait_ge(piece_lo, piece_no["wd", f, chunks[-1]] + 1)
                for t in range(TILES):
                    pe.wait_ge(act_ready, UNITS * f + 2 * chunks[-1] + t // 4 + 1)
                    if t >= 2:
                        pe.wait_ge(x_updated, base + t - 1)
                    at = slice(t * P, (t + 1) * P)
                    for c in chunks:
                        last = product(ps[:, 4 + t % 2, :], (act_hi[:, c % SLOTS, at], act_lo[:, c % SLOTS, at]),
                                       (wd_hi[:, c % FIRST, :], wd_lo[:, c % FIRST, :]),
                                       c == chunks[0], c == chunks[-1])
                    last.then_inc(down_done, 1)

            def ffn(f):
                for c in range(NCH):
                    if c == SLOTS:
                        down(f, 0)
                    for b in range(HALVES):
                        if c == 0:
                            for t in range(4 * b, 4 * b + 4):
                                turn(2 * f, t)
                        unit(f, c, b)
                down(f, 1)

            pe.wait_ge(ident_ready, 1)
            ffn(0)
            for t in range(TILES):
                turn(1, t)
            for t in range(TILES):
                pe.wait_ge(xt_ready, TILES + t + 1)
                pe.wait_ge(piece_lo, piece_no["qkv", 0, 5] + 1)
                at = slice(t * P, (t + 1) * P)
                for j in range(3):
                    if t >= 2:
                        pe.wait_ge(qkv_clipped, 3 * (t - 2) + j + 1)
                    cols = slice(j * D, (j + 1) * D)
                    for k in range(KC):
                        last = product(ps[:, 3 * (t % 2) + j, :], (xt_hi[:, k, at], xt_lo[:, k, at]),
                                       (qkv_hi[:, k, cols], qkv_lo[:, k, cols]), k == 0, k == KC - 1)
                    last.then_inc(qkv_done, 1)

            def fill(kind, j, G):
                n = fill_no[kind, j, G]
                if kind == "O":
                    pe.wait_ge(o_t_ready, G + 1)
                elif kind == "QB":
                    pe.wait_ge(shift_ready, G + 1)
                else:
                    pe.wait_ge(stack_ready, G + 1)
                if n >= 1:
                    pe.wait_ge(t_emptied, n)
                for t in range(QT):
                    if kind == "O":
                        source = o_t[:, G % 2, t * P:(t + 1) * P]
                    else:
                        stack = stack_k[:, G % 2, t] if kind == "K" else stack_q[:, G % 3, t]
                        source = stack[:, 2 * j:2 * j + 2, :].rearrange("p h r -> p (h r)").bitcast(F32)
                    last = nc.tensor.transpose(ps[:, TB, t * P:(t + 1) * P], source, ident[:, :])
                last.then_inc(t_filled, 1)

            def unit_bank_free(m):
                if m >= 2:
                    kind, i, j = unit_at[m - 2]
                    if kind == "A":
                        pe.wait_ge(a_emptied, A_UNITS * i + j + 1)
                    else:
                        pe.wait_ge(x_updated, FFN_UPDATES + QT * i + j + 1)

            def rows(turned, hh, at):
                return turned[64 * (hh % 2):64 * (hh % 2) + ROWS, hh // 2, at]

            def pass_a(G, n):
                m = unit_no["A", G, n]
                qt, heads = a_unit(n)
                width = P * (qt + 1)
                if n == 0:
                    pe.wait_ge(t_emptied, fill_no["QA", 1, G] + 1)
                unit_bank_free(m)
                for e, hh in enumerate(heads):
                    nc.tensor.matmul(ps[:, m % 2, e * width:(e + 1) * width],
                                     rows(qa_t[:, G % 2], hh, slice(qt * P, (qt + 1) * P)),
                                     rows(k_t[:, G % 4], hh, slice(0, width)),
                                     start=(e == 0), stop=False, skip_group_check=True)
                for e in range(len(heads)):
                    last = nc.tensor.matmul(ps[:, m % 2, (e + 1) * width - P:(e + 1) * width], ident_bf[:, :],
                                            mask_a[:, :], start=False, stop=(e == len(heads) - 1),
                                            skip_group_check=True)
                last.then_inc(a_filled, 1)

            def pass_b(G, n):
                idx = B_OPS * G + n
                kc, heads = b_op(n)
                if n == 0:
                    pe.wait_ge(t_emptied, fill_no["QB", 1, G] + 1)
                if idx >= 2:
                    pe.wait_ge(exp_done, idx - 1)
                width = S - kc * P
                for hh, bank, col in heads:
                    nc.tensor.matmul(ps[:, 2 + 2 * (idx % 2) + bank, col:col + width],
                                     rows(k_t[:, G % 4], hh, slice(kc * P, (kc + 1) * P)),
                                     rows(qb_t[:, G % 2], hh, slice(kc * P, S)),
                                     start=(col == 0), stop=False, skip_group_check=True)
                for hh, bank, col in heads:
                    last = nc.tensor.matmul(ps[:, 2 + 2 * (idx % 2) + bank, col:col + P], ident_bf[:, :],
                                            mask_b[:, :], start=False, stop=True, skip_group_check=True)
                last.then_inc(b_filled, 1)

            def probs_v(G, n):
                idx = B_OPS * G + n
                b, g = G // GROUPS, G % GROUPS
                kc, heads = b_op(n)
                if n == 0:
                    pe.wait_ge(pv_cleared, 1)
                    if G >= 1:
                        pe.wait_ge(o_t_ready, G)
                pe.wait_ge(exp_done, idx + 1)
                width = S - kc * P
                for e, (hh, _, _) in enumerate(heads):
                    last = nc.tensor.matmul(ps[32 * hh:32 * hh + VW, PV, kc * P:S], vext[:, b, kc, GH * g + hh, :],
                                            probs[:, idx % 3, e * width:(e + 1) * width],
                                            start=(kc == 0), stop=(kc == QT - 1), skip_group_check=True,
                                            tile_position=(0, 32 * hh))
                last.then_inc(pv_step, 1)

            pe.wait_ge(masks_ready, 3)
            pe.wait_ge(vones_ready, 1)
            pe.wait_ge(qkv_clipped, 3 * TILES)
            pe.wait_ge(qk_ready, 2 * TILES)
            for s in STEPS:
                for i in range(B_OPS):
                    if 0 <= s - 2 < NG:
                        pass_b(s - 2, i)
                    for n in (2 * i, 2 * i + 1):
                        if 0 <= s < NG and n < A_UNITS:
                            pass_a(s, n)
                    if i >= 1 and 0 <= s - 2 < NG:
                        probs_v(s - 2, i - 1)
                    for kind, j, G in fills_at(s, i):
                        fill(kind, j, G)
                if 0 <= s - 2 < NG:
                    probs_v(s - 2, B_OPS - 1)
                if outproj_at(s):
                    b, t = outproj_at(s)
                    n, u = fill_no["AT", b, t], unit_no["Y", b, t]
                    pe.wait_ge(t_emptied, n)
                    for k in range(KC):
                        last = nc.tensor.transpose(ps[:, TB, k * P:(k + 1) * P], attn[:, b, t, k * P:(k + 1) * P],
                                                   ident[:, :])
                    last.then_inc(t_filled, 1)
                    m = b * QT + t
                    pe.wait_ge(t_emptied, n + 1)
                    pe.wait_ge(piece_lo, piece_no["wo", 0, 1] + 1)
                    unit_bank_free(u)
                    for k in range(KC):
                        last = product(ps[:, u % 2, :], (at_hi[:, m % 2, k, :], at_lo[:, m % 2, k, :]),
                                       (wo_hi[:, k, :], wo_lo[:, k, :]), k == 0, k == KC - 1)
                    last.then_inc(a_filled, 1)
            ffn(1)


def contraction_rows():
    slope = (1.0 / np.power(2.0, np.arange(1, H + 1) * (8.0 / H))).astype(np.float32)
    scale = np.exp2(np.floor(np.log2(slope)) - 11).astype(np.float32)
    hi = (np.round(slope / scale) * scale).astype(np.float32)
    lo = slope - hi
    pos = (np.arange(QT)[None, :] * P + np.arange(P)[:, None]).astype(np.float32)[:, :, None]
    rows_q = (hi, -pos, lo, -pos, 0.0, 0.0)
    rows_k = (pos, hi, pos, lo, 1.0, 1.0)
    return [np.ascontiguousarray(np.stack([np.broadcast_to(r, (P, QT, H)) for r in rows], -1), np.float32)
            for rows in (rows_q, rows_k)]


def kernel(L0_attn_hidden_states, L0_attn_w_qkv, L0_attn_q_ln_w, L0_attn_q_ln_b, L0_attn_k_ln_w, L0_attn_k_ln_b,
           L0_attn_w_out, L0_ffn_ln_w, L0_ffn_gate_w, L0_ffn_up_w, L0_ffn_down_w):
    import concourse.bacc as bacc
    from concourse.bass_utils import run_bass_kernel_spmd

    def turned(w, n):
        w = np.asarray(w)
        return w.reshape(w.shape[0] // n, n, KC, P).transpose(0, 3, 2, 1)

    w_gu = np.stack([turned(L0_ffn_gate_w, P), turned(L0_ffn_up_w, P)], 2)
    con_q, con_k = contraction_rows()
    arrays = {
        "x_in": np.asarray(L0_attn_hidden_states).reshape(B * S, D),
        "w_gu": w_gu.reshape(NCH, P, PIECE),
        "w_down": np.asarray(L0_ffn_down_w).T.reshape(NCH, P, D),
        "w_qkv": turned(L0_attn_w_qkv, 256).reshape(6, P, PIECE),
        "w_out": turned(L0_attn_w_out, 256).reshape(2, P, PIECE),
        "ln_w": np.asarray(L0_ffn_ln_w).reshape(1, D),
        "q_w": np.asarray(L0_attn_q_ln_w).reshape(1, D),
        "q_b": np.asarray(L0_attn_q_ln_b).reshape(1, D),
        "k_w": np.asarray(L0_attn_k_ln_w).reshape(1, D),
        "k_b": np.asarray(L0_attn_k_ln_b).reshape(1, D),
        "con_q": con_q,
        "con_k": con_k,
    }
    arrays = {name: np.ascontiguousarray(a) for name, a in arrays.items()}
    nc = bacc.Bacc("TRN2", target_bir_lowering=False, num_devices=1)
    ins = [nc.dram_tensor(name, a.shape, F32, kind="ExternalInput").ap() for name, a in arrays.items()]
    out = nc.dram_tensor("out", (B * S, D), F32, kind="ExternalOutput").ap()
    build(nc, *ins, out)
    got = run_bass_kernel_spmd(nc, [arrays], core_ids=[0])
    return got.results[0]["out"].reshape(B, S, D)
```

```python
from contextlib import ExitStack

import numpy as np

import concourse.bass as bass
from concourse import mybir

ALU = mybir.AluOpType
ACT = mybir.ActivationFunctionType
AX = mybir.AxisListType
F32 = mybir.dt.float32
F32R = mybir.dt.float32r
BF16 = mybir.dt.bfloat16

P = 128
B, S, D = 2, 512, 512
I = 1792
H = 32
HD = D // H
KC = D // P
TILES = B * S // P
NCH = I // P
FIRST = 7
AHEAD = 2
SLOTS = FIRST + 1
HALVES = B * S // 512
UNITS = NCH * HALVES
EPS = 1e-5
CLIP = 8.0
MASKED = -3.0e38

RAW = 3
PIECE = KC * 2 * P

GH = 4
GROUPS = H // GH
NG = B * GROUPS
QT = S // P
ROWS = 64
CON = 6
A_UNITS = 12
B_OPS = 6
WARM = 3
QC = 3
VW = HD + 1


QK_PIECES = [("qk", 0, j) for j in range(4)]
V_PIECES = [("v", 0, j) for j in range(2)]
WO_PIECES = [("wo", 0, j) for j in range(2)]


def ffn_pieces(f):
    def gu(c):
        return ("gu", f, c)

    def wd(c):
        return ("wd", f, c)

    after = {-1: [gu(0), gu(1), wd(0)]}
    for c in range(5):
        after[c] = [gu(c + 2), wd(c + 1)]
    after[5] = [gu(7), wd(6)]
    after[6] = [gu(8)]
    after[7] = [gu(9)]
    after[8] = [gu(10), wd(7), wd(8)]
    after[9] = [gu(11), wd(9)]
    after[10] = [gu(12), wd(10)]
    after[11] = [gu(13), wd(11)]
    after[12] = [wd(12), wd(13)]
    after[13] = []
    return after


def fills_at(s, i):
    out = []
    if i == 0:
        out = [("O", 0, s - 3)]
    elif i == 1:
        out = [("QB", 0, s - 1)]
    elif i == 2:
        out = [("QB", 1, s - 1)]
    elif i == 3:
        out = [("K", 0, s + 1)]
    elif i == 4:
        out = [("K", 1, s + 1)]
    elif i == 5:
        out = [("QA", 0, s + 1), ("QA", 1, s + 1)]
    return [f for f in out if 0 <= f[2] < NG]


def outproj_at(s):
    for b in range(B):
        if s == (b + 1) * GROUPS - 1 + 3:
            return b
    return None


STEPS = range(-1, NG + 3)


def number_attention():
    fills, units = {}, {}
    for s in STEPS:
        for i in range(B_OPS):
            for n in (2 * i, 2 * i + 1):
                if 0 <= s < NG and n < A_UNITS:
                    units[("A", s, n)] = len(units)
            for f in fills_at(s, i):
                fills[f] = len(fills)
        b = outproj_at(s)
        if b is not None:
            for t in range(QT):
                fills["AT", b, t] = len(fills)
                units["Y", b, t] = len(units)
    return fills, units


def a_unit(n):
    if n < 4:
        return n // 2, [n % 2, n % 2 + 2]
    return 2 + (n - 4) // GH, [(n - 4) % GH]


def maxima_taken(G, n):
    return GH * QT * G + (2 * (n + 1) if n < 4 else n + 5)


def b_op(n):
    if n < 4:
        kc, first = n // 2, 2 * (n % 2)
        return kc, [(first, 0, 0), (first + 1, 1, 0)]
    kc = n - 2
    return kc, [(hh, hh % 2, (S - kc * P) * (hh // 2)) for hh in (0, 2, 1, 3)]


def build(nc, x_in, w_gu, w_down, w_qkv, w_out, ln_w, q_w, q_b, k_w, k_b, con_q, con_k, out):
    persistent = ExitStack()
    with persistent:
        def sem(name):
            return persistent.enter_context(nc.semaphore(name))

        def allocate(stack, name, shape, dt):
            return stack.enter_context(nc.sbuf_tensor(name, shape, dt))

        def sb(name, shape, dt=F32):
            return allocate(persistent, name, shape, dt)

        x = sb("x", [P, TILES, D])
        raw = sb("raw", [P, RAW, PIECE])
        lnw_row = sb("lnw_row", [P, D])
        ident = sb("ident", [P, P])
        ident_bf = sb("ident_bf", [P, P], BF16)
        mask_a = sb("mask_a", [P, S], BF16)
        mask_b = sb("mask_b", [P, P], BF16)
        y = sb("y", [P, 2, D])
        ident_r = sb("ident_r", [P, P], F32R)
        stats = sb("stats", [P, 2, 6])
        mean_var = sb("mean_var", [P, 2, 2])
        power = sb("power", [P, 1])
        rstd = sb("rstd", [P, 2, 1])
        rms = sb("rms", [P, 2, 1])
        q_stats = sb("q_stats", [P, 2, 6])
        q_mean_var = sb("q_mean_var", [P, 4, 2])
        q_rstd = sb("q_rstd", [P, 4, 1])
        row_max = sb("row_max", [P, 2, QT, GH])
        rsum = sb("rsum", [P, QT, GH])

        far = ExitStack()
        xt_hi = far.enter_context(nc.sbuf_tensor("xt_hi", [P, KC, B * S], F32R, side="right"))
        xt_lo = far.enter_context(nc.sbuf_tensor("xt_lo", [P, KC, B * S], F32R, side="right"))
        qk_hi = far.enter_context(nc.sbuf_tensor("qk_hi", [P, KC, 2 * D], F32R, side="right"))
        qk_lo = far.enter_context(nc.sbuf_tensor("qk_lo", [P, KC, 2 * D], F32R, side="right"))
        far.close()

        with ExitStack() as ffn_stage:
            wd_hi = allocate(ffn_stage, "wd_hi", [P, FIRST, D], F32R)
            wd_lo = allocate(ffn_stage, "wd_lo", [P, FIRST, D], F32R)
            act_hi = allocate(ffn_stage, "act_hi", [P, SLOTS, B * S], F32R)
            act_lo = allocate(ffn_stage, "act_lo", [P, SLOTS, B * S], F32R)
            gu_hi = allocate(ffn_stage, "gu_hi", [P, 2, 2, KC, P], F32R)
            gu_lo = allocate(ffn_stage, "gu_lo", [P, 2, 2, KC, P], F32R)
            silu_g = allocate(ffn_stage, "silu_g", [P, 2, 512], F32)
            act_f = allocate(ffn_stage, "act_f", [P, 2, 512], F32)

        mid = ExitStack()
        qn = allocate(mid, "qn", [P, B, QT, D], F32)
        kn = allocate(mid, "kn", [P, B, QT, D], F32)
        vext = allocate(mid, "vext", [P, B, QT, H, VW], F32)
        cq = allocate(mid, "cq", [P, QT, H, CON], F32)
        ck = allocate(mid, "ck", [P, QT, H, CON], F32)
        stack_k = allocate(mid, "stack_k", [P, 2, QT, GH, ROWS], F32R)
        stack_q = allocate(mid, "stack_q", [P, 3, QT, GH, ROWS], F32R)
        with ExitStack() as qkv_stage:
            v_hi = allocate(qkv_stage, "v_hi", [P, KC, D], F32R)
            v_lo = allocate(qkv_stage, "v_lo", [P, KC, D], F32R)
            wb = allocate(qkv_stage, "wb", [P, 4, D], F32)
            qc = allocate(qkv_stage, "qc", [P, QC, D], F32)

        with ExitStack() as att:
            attn = allocate(att, "attn", [P, QT, D], F32)
            o_t = allocate(att, "o_t", [P, S], F32)
            probs = allocate(att, "probs", [P, 3, 1024], F32)
            at_hi = allocate(att, "at_hi", [P, 2, KC, P], F32R)
            at_lo = allocate(att, "at_lo", [P, 2, KC, P], F32R)
            k_t = allocate(att, "k_t", [P, 4, GH, S], F32R)
            qa_t = allocate(att, "qa_t", [P, 2, 2, S], F32R)
            qb_t = allocate(att, "qb_t", [P, 2, 2, S], F32R)
            wo_hi = allocate(att, "wo_hi", [P, KC, D], F32R)
            wo_lo = allocate(att, "wo_lo", [P, KC, D], F32R)
        mid.close()

        ps = persistent.enter_context(nc.psum_tensor("ps", [P, 8, 512], F32))
        PV, TB = 6, 7

        x_loaded = [sem(f"x_loaded{t}") for t in range(TILES)]
        rows_loaded = sem("rows_loaded")
        cons_loaded = sem("cons_loaded")
        wb_loaded = sem("wb_loaded")
        warmed = sem("warmed")
        k_zeroed = sem("k_zeroed")
        raw_loaded = [sem(f"raw_loaded{n}") for n in range(RAW)]
        piece_hi = sem("piece_hi")
        piece_lo = sem("piece_lo")
        ident_ready = sem("ident_ready")
        masks_ready = sem("masks_ready")
        dve_step = sem("dve_step")
        pool_step = sem("pool_step")
        var_ready = sem("var_ready")
        rstd_ready = sem("rstd_ready")
        norm_ready = sem("norm_ready")
        norm_turned = sem("norm_turned")
        xt_hi_ready = sem("xt_hi_ready")
        xt_ready = sem("xt_ready")
        gate_done = sem("gate_done")
        up_done = sem("up_done")
        silu_done = sem("silu_done")
        act_f_ready = sem("act_f_ready")
        act_hi_ready = sem("act_hi_ready")
        act_ready = sem("act_ready")
        down_done = sem("down_done")
        x_updated = sem("x_updated")
        qkv_done = sem("qkv_done")
        qkv_clipped = sem("qkv_clipped")
        q_var_ready = sem("q_var_ready")
        q_rstd_ready = sem("q_rstd_ready")
        qk_ready = sem("qk_ready")
        vones_ready = sem("vones_ready")
        stack_ready = sem("stack_ready")
        pv_cleared = sem("pv_cleared")
        t_filled = sem("t_filled")
        t_emptied = sem("t_emptied")
        a_filled = sem("a_filled")
        a_emptied = sem("a_emptied")
        shift_ready = sem("shift_ready")
        b_filled = sem("b_filled")
        exp_done = sem("exp_done")
        pv_step = sem("pv_step")
        o_t_ready = sem("o_t_ready")
        at_hi_ready = sem("at_hi_ready")
        stored = sem("stored")

        pieces = []
        for f in range(2):
            after = ffn_pieces(f)
            pieces += [p for c in range(-1, NCH) for p in after[c]]
            if f == 0:
                pieces += QK_PIECES + V_PIECES + WO_PIECES
        piece_no = {p: n for n, p in enumerate(pieces)}
        fill_no, unit_no = number_attention()
        unit_at = {n: unit for unit, n in unit_no.items()}
        fill_at = {n: fill for fill, n in fill_no.items()}
        emptied_after, count = {}, 0
        for fill in fill_no:
            count += 2 if fill[0] == "K" else 1
            emptied_after[fill] = count
        FFN_UPDATES = 2 * TILES
        ATT_UPDATES = TILES

        def updates_before(f):
            return f * (FFN_UPDATES + ATT_UPDATES)

        def turn_bank(phase, t):
            return (4 if phase == 2 else 6) + t % 2

        def piece_source(p):
            kind, _, c = p
            if kind == "gu":
                return w_gu[c], PIECE
            if kind == "wd":
                return w_down[c], D
            return {"qk": w_qkv[c], "v": w_qkv[4 + c % 2], "wo": w_out[c % 2]}[kind], PIECE

        def piece_views(p):
            kind, _, c = p
            slot = raw[:, piece_no[p] % RAW, :]
            if kind == "gu":
                v = slot.rearrange("p (a k n) -> p a k n", a=2, k=KC)
                return v, gu_hi[:, c % 2], gu_lo[:, c % 2]
            if kind == "wd":
                return slot[:, 0:D], wd_hi[:, c % FIRST, :], wd_lo[:, c % FIRST, :]
            v = slot.rearrange("p (k n) -> p k n", k=KC)
            hi, lo = {"qk": (qk_hi, qk_lo), "v": (v_hi, v_lo), "wo": (wo_hi, wo_lo)}[kind]
            return v, hi[:, :, 256 * c:256 * c + 256], lo[:, :, 256 * c:256 * c + 256]

        block = persistent.enter_context(nc.Block())

        @block.sync
        def _(sp):
            for t in range(TILES):
                sp.dma_start(x[:, t, :], x_in[t * P:(t + 1) * P, :]).then_inc(x_loaded[t], 16)
                if t == 3:
                    sp.dma_start(lnw_row[:, :], ln_w.broadcast_to([P, D])).then_inc(rows_loaded, 16)
                if 3 <= t < 3 + RAW:
                    source, n = piece_source(pieces[t - 3])
                    sp.dma_start(raw[:, t - 3, 0:n], source).then_inc(raw_loaded[t - 3], 16)
            for n, p in enumerate(pieces):
                if n < RAW:
                    continue
                if p == WO_PIECES[1]:
                    sp.wait_ge(x_updated, FFN_UPDATES)
                    for j, row in enumerate((q_w, q_b, k_w, k_b)):
                        sp.dma_start(wb[:, j, :], row.broadcast_to([P, D])).then_inc(wb_loaded, 16)
                    sp.dma_start(cq[:, :, :, :], con_q).then_inc(cons_loaded, 16)
                    sp.dma_start(ck[:, :, :, :], con_k).then_inc(cons_loaded, 16)
                sp.wait_ge(piece_lo, n - RAW + 1)
                source, size = piece_source(p)
                sp.dma_start(raw[:, n % RAW, 0:size], source).then_inc(raw_loaded[n % RAW], 16)
            base = updates_before(1) + TILES
            for t in range(TILES):
                sp.wait_ge(x_updated, base + t + 1)
                sp.dma_start(out[t * P:(t + 1) * P, :], x[:, t, :]).then_inc(stored, 16)
            sp.wait_ge(stored, 16 * TILES)

        @block.gpsimd
        def _(pool):
            steps = [0]

            def link(ins):
                steps[0] += 1
                ins.then_inc(pool_step, 1)
                pool.wait_ge(pool_step, steps[0])

            link(nc.gpsimd.memset(ident[:, :], 0.0))
            link(nc.gpsimd.affine_select(out=ident[:, :], in_=ident[:, :], compare_op=ALU.not_equal, fill=1.0,
                                         base=0, pattern=[[-1, P]], channel_multiplier=1))
            nc.gpsimd.memset(power[:, :], -0.5).then_inc(ident_ready, 1)
            pool.wait_ge(ident_ready, 1)

            nc.gpsimd.tensor_copy(ident_bf[:, :], ident[:, :]).then_inc(masks_ready, 1)
            nc.gpsimd.tensor_copy(ident_r[:, :], ident[:, :]).then_inc(masks_ready, 1)
            link(nc.gpsimd.memset(mask_a[:, :], 0.0))
            link(nc.gpsimd.memset(mask_b[:, :], 0.0))
            nc.gpsimd.affine_select(out=mask_a[:, :], in_=mask_a[:, :], compare_op=ALU.is_ge, fill=MASKED,
                                    base=S - P, pattern=[[-1, S]], channel_multiplier=1).then_inc(masks_ready, 1)
            nc.gpsimd.affine_select(out=mask_b[:, :], in_=mask_b[:, :], compare_op=ALU.is_ge, fill=MASKED, base=0,
                                    pattern=[[1, P]], channel_multiplier=-1).then_inc(masks_ready, 1)

            def inverse_root(dst, src, scale):
                link(nc.gpsimd.tensor_scalar(dst, src, scale, EPS, ALU.mult, ALU.add))
                return nc.gpsimd.tensor_tensor(dst, dst, power[:, :], ALU.pow)

            def norm_tile(phase, t):
                n = phase * TILES + t
                r, m, var = rstd[:, n % 2, :], rms[:, n % 2, :], mean_var[:, n % 2, 1:2]
                pool.wait_ge(var_ready, n + 1)
                if phase == 1:
                    inverse_root(r, var, 1.0).then_inc(rstd_ready, 1)
                else:
                    link(inverse_root(r, var, 1.0))
                    link(nc.gpsimd.tensor_tensor(m, r, r, ALU.mult))
                    link(nc.gpsimd.tensor_tensor(m, m, var, ALU.mult))
                    link(inverse_root(m, m, 1.0))
                    nc.gpsimd.tensor_tensor(r, r, m, ALU.mult).then_inc(rstd_ready, 1)

            def split_low(p):
                v, hi, lo = piece_views(p)
                pool.wait_ge(piece_hi, piece_no[p] + 1)
                nc.gpsimd.tensor_tensor(lo, v, hi.bitcast(F32), ALU.subtract).then_inc(piece_lo, 1)

            def ffn(f):
                after = ffn_pieces(f)
                for t in range(TILES):
                    norm_tile(2 * f, t)
                    if t == 3:
                        for p in after[-1]:
                            split_low(p)
                for c in range(NCH):
                    for b in range(HALVES):
                        u = UNITS * f + 2 * c + b
                        pool.wait_ge(act_hi_ready, u + 1)
                        at = slice(512 * b, 512 * b + 512)
                        nc.gpsimd.tensor_tensor(act_lo[:, c % SLOTS, at], act_f[:, u % 2, :],
                                                act_hi[:, c % SLOTS, at].bitcast(F32),
                                                ALU.subtract).then_inc(act_ready, 1)
                    for p in after[c]:
                        split_low(p)

            def stack_group(G):
                b, g = G // GROUPS, G % GROUPS
                sk, sq = stack_k[:, G % 2], stack_q[:, G % 3]
                heads = slice(GH * g, GH * g + GH)
                q = qn[:, b].rearrange("p t (h d) -> p t h d", d=HD)[:, :, heads, :]
                k = kn[:, b].rearrange("p t (h d) -> p t h d", d=HD)[:, :, heads, :]
                if G == 0:
                    pool.wait_ge(cons_loaded, 16 * 2)
                pool.wait_ge(qk_ready, TILES * (b + 1))
                if G >= 2:
                    pool.wait_ge(t_filled, fill_no["K", 1, G - 2] + 1)
                nc.gpsimd.tensor_copy(sk[:, :, :, 16:32], k)
                nc.gpsimd.tensor_copy(sk[:, :, :, 0:CON], ck[:, :, heads, :])
                link(nc.gpsimd.tensor_copy(sk[:, :, :, 32:48], k))
                nc.gpsimd.tensor_tensor(sk[:, :, :, 48:64], k, sk[:, :, :, 32:48].bitcast(F32), ALU.subtract)
                if G >= 3:
                    pool.wait_ge(t_filled, fill_no["QB", 1, G - 3] + 1)
                nc.gpsimd.tensor_copy(sq[:, :, :, 16:32], q)
                nc.gpsimd.tensor_copy(sq[:, :, :, 0:CON], cq[:, :, heads, :])
                link(nc.gpsimd.tensor_copy(sq[:, :, :, 48:64], q))
                nc.gpsimd.tensor_tensor(sq[:, :, :, 32:48], q, sq[:, :, :, 48:64].bitcast(F32),
                                        ALU.subtract).then_inc(stack_ready, 1)

            ffn(0)
            for p in QK_PIECES:
                split_low(p)
            for t in range(TILES):
                norm_tile(1, t)
            pool.wait_ge(x_updated, FFN_UPDATES)
            for p in V_PIECES:
                split_low(p)
            link(nc.gpsimd.memset(stack_k[:, :, :, :, :].bitcast(F32), 0.0))
            link(nc.gpsimd.memset(stack_q[:, :, :, :, :].bitcast(F32), 0.0))
            for n in range(2 * TILES):
                pool.wait_ge(q_var_ready, n + 1)
                inverse_root(q_rstd[:, n % 4, :], q_mean_var[:, n % 4, 1:2], 1.0).then_inc(q_rstd_ready, 1)
                if n in (11, 13):
                    stack_group(n // 2 - 5)
            pool.wait_ge(qkv_done, 3 * TILES)
            for n in range(4):
                nc.gpsimd.memset(k_t[:, n].bitcast(F32), 0.0).then_inc(k_zeroed, 1)
            for G in range(2, NG):
                stack_group(G)
                if G == 3:
                    for p in WO_PIECES:
                        split_low(p)
            ffn(1)

        @block.scalar
        def _(act):
            def turn_high(phase, t):
                n = phase * TILES + t
                act.wait_ge(norm_turned, n + 1)
                nc.scalar.activation(xt_hi[:, :, t * P:(t + 1) * P],
                                     ps[:, turn_bank(phase, t), :].rearrange("p (k n) -> p k n", k=KC),
                                     ACT.Copy).then_inc(xt_hi_ready, 1)

            def norms(phase):
                for t in range(TILES):
                    turn_high(phase, t)

            def high(u):
                c, b = (u % UNITS) // 2, u % 2
                act.wait_ge(act_f_ready, u + 1)
                if c >= SLOTS:
                    act.wait_ge(down_done, FFN_UPDATES * (u // UNITS) + TILES)
                nc.scalar.activation(act_hi[:, c % SLOTS, 512 * b:512 * b + 512], act_f[:, u % 2, :],
                                     ACT.Copy).then_inc(act_hi_ready, 1)

            def ffn(f):
                for u in range(UNITS * f, UNITS * f + UNITS):
                    act.wait_ge(gate_done, u + 1)
                    if u >= 2:
                        act.wait_ge(act_f_ready, u - 1)
                    nc.scalar.activation(silu_g[:, u % 2, :], ps[:, u % 2, :], ACT.Silu).then_inc(silu_done, 1)
                    if u > UNITS * f:
                        high(u - 1)
                high(UNITS * f + UNITS - 1)

            norms(0)
            ffn(0)
            norms(1)

            def exp(G, n):
                idx = B_OPS * G + n
                kc, heads = b_op(n)
                bank = 2 + 2 * (idx % 2)
                act.wait_ge(b_filled, idx + 1)
                if idx >= 3:
                    act.wait_ge(pv_step, idx - 2)
                width = (S - kc * P) * len(heads) // 2
                nc.scalar.activation(probs[:, idx % 3, 0:2 * width].rearrange("p (a n) -> p a n", a=2),
                                     ps[:, bank:bank + 2, 0:width], ACT.Exp).then_inc(exp_done, 1)

            def evacuate(kind, j, G):
                n = fill_no[kind, j, G]
                act.wait_ge(t_filled, n + 1)
                if kind == "K":
                    if G < 4:
                        act.wait_ge(k_zeroed, G + 1)
                    nc.scalar.activation(k_t[0:ROWS, G % 4, 2 * j, :], ps[0:ROWS, TB, :],
                                         ACT.Copy).then_inc(t_emptied, 1)
                else:
                    dst = {"QA": qa_t, "QB": qb_t}[kind][:, G % 2, j, :]
                    nc.scalar.activation(dst, ps[:, TB, :], ACT.Copy).then_inc(t_emptied, 1)

            for s in STEPS:
                for i in range(B_OPS):
                    if 0 <= s - 2 < NG:
                        exp(s - 2, i)
                    for kind, j, G in fills_at(s, i):
                        if kind != "O":
                            evacuate(kind, j, G)
                if 0 <= s - 2 < NG:
                    G = s - 2
                    act.wait_ge(pv_step, B_OPS * G + B_OPS)
                    if G >= 1:
                        act.wait_ge(t_filled, fill_no["O", 0, G - 1] + 1)
                    nc.scalar.activation(o_t[:, :], ps[:, PV, :], ACT.Copy).then_inc(o_t_ready, 1)
                for t in range(QT) if outproj_at(s) is not None else ():
                    b = outproj_at(s)
                    m = b * QT + t
                    act.wait_ge(t_filled, fill_no["AT", b, t] + 1)
                    if m >= 2:
                        act.wait_ge(a_filled, unit_no["Y", (m - 2) // QT, (m - 2) % QT] + 1)
                    nc.scalar.activation(at_hi[:, m % 2], ps[:, TB, :].rearrange("p (k n) -> p k n", k=KC),
                                         ACT.Copy).then_inc(at_hi_ready, 1)
            norms(2)
            ffn(1)

        @block.vector
        def _(dve):
            steps = [0]

            def link(ins):
                steps[0] += 1
                ins.then_inc(dve_step, 1)
                dve.wait_ge(dve_step, steps[0])

            def norm_stats(phase, t):
                n = phase * TILES + t
                if phase == 0:
                    dve.wait_ge(x_loaded[t], 16)
                else:
                    dve.wait_ge(x_updated, (FFN_UPDATES if phase == 1 else updates_before(1)) - TILES + t + 1)
                if n >= 2:
                    dve.wait_ge(rstd_ready, n - 1)
                link(nc.vector.bn_stats(stats[:, n % 2, :], x[:, t, :]))
                nc.vector.bn_aggr(mean_var[:, n % 2, :], stats[:, n % 2, :]).then_inc(var_ready, 1)

            def norm_apply(phase, t):
                n = phase * TILES + t
                dve.wait_ge(rstd_ready, n + 1)
                dve.wait_ge(var_ready, n + 1)
                if n >= 2:
                    dve.wait_ge(norm_turned, n - 1)
                ins = nc.vector.tensor_scalar(y[:, n % 2, :], x[:, t, :], mean_var[:, n % 2, 0:1],
                                              rstd[:, n % 2, :], ALU.subtract, ALU.mult)
                if phase != 1:
                    link(ins)
                    if phase == 0 and t == 0:
                        dve.wait_ge(rows_loaded, 16)
                    ins = nc.vector.tensor_tensor(y[:, n % 2, :], y[:, n % 2, :], lnw_row[:, :], ALU.mult)
                ins.then_inc(norm_ready, 1)

            def turn_low(phase, t):
                n = phase * TILES + t
                at = slice(t * P, (t + 1) * P)
                dve.wait_ge(xt_hi_ready, n + 1)
                nc.vector.tensor_tensor(xt_lo[:, :, at], ps[:, turn_bank(phase, t), :].rearrange("p (k n) -> p k n", k=KC),
                                        xt_hi[:, :, at].bitcast(F32), ALU.subtract).then_inc(xt_ready, 1)

            def split_high(p):
                kind, f, c = p
                n = piece_no[p]
                v, hi, _ = piece_views(p)
                dve.wait_ge(raw_loaded[n % RAW], 16 * (n // RAW + 1))
                if f == 1 and c < 2:
                    dve.wait_ge(pv_step, B_OPS * NG)
                if kind == "gu" and c >= 2:
                    dve.wait_ge(up_done, UNITS * f + 2 * (c - 2) + 2)
                if kind == "wd" and c >= FIRST:
                    dve.wait_ge(down_done, FFN_UPDATES * f + TILES)
                nc.vector.tensor_copy(hi, v).then_inc(piece_hi, 1)

            def norms(phase, before=None, pieces_at=()):
                for t in range(TILES + 2):
                    if t < TILES:
                        if before:
                            before(t)
                        norm_stats(phase, t)
                    if 1 <= t <= TILES:
                        norm_apply(phase, t - 1)
                    if t >= 2:
                        turn_low(phase, t - 2)
                    if t == 3:
                        for p in pieces_at:
                            split_high(p)

            def x_update(n, bank, scale):
                t = n % TILES
                if n >= TILES:
                    dve.wait_ge(x_updated, n - TILES + 1)
                nc.vector.scalar_tensor_tensor(out=x[:, t, :], in0=ps[:, bank, :], scalar=scale, in1=x[:, t, :],
                                               op0=ALU.mult, op1=ALU.add).then_inc(x_updated, 1)

            def ffn(f):
                after = ffn_pieces(f)
                base = updates_before(f)

                def out_tile(r, t):
                    dve.wait_ge(down_done, FFN_UPDATES * f + TILES * r + t + 1)
                    x_update(base + TILES * r + t, 4 + t % 2, 0.5)

                for c in range(NCH):
                    if c == SLOTS:
                        for t in range(TILES):
                            out_tile(0, t)
                    for b in range(HALVES):
                        u = UNITS * f + 2 * c + b
                        dve.wait_ge(silu_done, u + 1)
                        dve.wait_ge(up_done, u + 1)
                        if u >= 2:
                            dve.wait_ge(act_ready, u - 1)
                        nc.vector.tensor_tensor(act_f[:, u % 2, :], ps[:, 2 + u % 2, :], silu_g[:, u % 2, :],
                                                ALU.mult).then_inc(act_f_ready, 1)
                    for p in after[c]:
                        split_high(p)
                if f == 0:
                    dve.wait_ge(act_ready, UNITS)
                    for p in QK_PIECES:
                        split_high(p)
                    norms(1, before=lambda t: out_tile(1, t))
                else:
                    for t in range(TILES):
                        out_tile(1, t)

            norms(0, pieces_at=ffn_pieces(0)[-1])
            ffn(0)
            dve.wait_ge(x_updated, FFN_UPDATES)
            for p in V_PIECES:
                split_high(p)
            nc.vector.memset(vext[:, :, :, :, HD:VW], 1.0).then_inc(vones_ready, 1)
            dve.wait_ge(wb_loaded, 16 * 4)
            link(nc.vector.tensor_scalar(wb[:, 0:2, :], wb[:, 0:2, :], float(HD) ** -0.5, None, ALU.mult))
            for t in range(TILES):
                for j in range(2):
                    n = 2 * t + j
                    dve.wait_ge(qkv_done, 3 * t + j + 1)
                    link(nc.vector.tensor_scalar(qc[:, n % QC, :], ps[:, 3 * (t % 2) + j, :], CLIP, -CLIP,
                                                 ALU.min, ALU.max))
                    link(nc.vector.bn_stats(q_stats[:, j, :], qc[:, n % QC, :]))
                    link(nc.vector.bn_aggr(q_mean_var[:, n % 4, :], q_stats[:, j, :]))
                    nc.vector.scalar_tensor_tensor(out=qc[:, n % QC, :], in0=qc[:, n % QC, :],
                                                   scalar=q_mean_var[:, n % 4, 0:1], in1=wb[:, 2 * j, :],
                                                   op0=ALU.subtract, op1=ALU.mult).then_inc(q_var_ready, 1)
                dve.wait_ge(qkv_done, 3 * t + 3)
                nc.vector.tensor_scalar(vext[:, t // QT, t % QT, :, 0:HD],
                                        ps[:, 3 * (t % 2) + 2, :].rearrange("p (h d) -> p h d", d=HD),
                                        CLIP, -CLIP, ALU.min, ALU.max).then_inc(qkv_clipped, 1)
                for j in range(2):
                    n = 2 * t + j
                    dve.wait_ge(q_rstd_ready, n + 1)
                    dve.wait_ge(q_var_ready, n + 1)
                    nc.vector.scalar_tensor_tensor(out=(qn, kn)[j][:, t // QT, t % QT, :], in0=qc[:, n % QC, :],
                                                   scalar=q_rstd[:, n % 4, :], in1=wb[:, 2 * j + 1, :],
                                                   op0=ALU.mult, op1=ALU.add).then_inc(qk_ready, 1)

            dve.wait_ge(qk_ready, 2 * TILES)
            dve.wait_ge(masks_ready, 4)

            def take_max(G, n):
                m = unit_no["A", G, n]
                qt, heads = a_unit(n)
                width = P * (qt + 1)
                dve.wait_ge(a_filled, m + 1)
                for e, hh in enumerate(heads):
                    taken = maxima_taken(G, n) - len(heads) + e
                    if taken >= 2:
                        dve.wait_ge(a_emptied, taken - 1)
                    nc.vector.tensor_tensor_reduce(
                        out=y[:, taken % 2, 0:width], in0=ps[:, m % 2, e * width:(e + 1) * width],
                        in1=mask_a[:, S - width:S], scale=1.0, scalar=MASKED, op0=ALU.add, op1=ALU.max,
                        accum_out=row_max[:, G % 2, qt, hh:hh + 1]).then_inc(a_emptied, 1)

            def shift(G):
                sq = stack_q[:, G % 3]
                m = row_max[:, G % 2]
                dve.wait_ge(a_emptied, maxima_taken(G, A_UNITS - 1))
                dve.wait_ge(t_filled, fill_no["QA", 1, G] + 1)
                link(nc.vector.tensor_copy(sq[:, :, :, 4], m))
                nc.vector.tensor_tensor(sq[:, :, :, 5], m, sq[:, :, :, 4].bitcast(F32),
                                        ALU.subtract).then_inc(shift_ready, 1)

            for s in STEPS:
                for i in range(B_OPS):
                    for n in (2 * i, 2 * i + 1):
                        if 0 <= s < NG and n < A_UNITS:
                            take_max(s, n)
                    for kind, j, G in fills_at(s, i):
                        if kind == "K":
                            dve.wait_ge(t_filled, fill_no[kind, j, G] + 1)
                            if G < 4:
                                dve.wait_ge(k_zeroed, G + 1)
                            nc.vector.tensor_copy(k_t[ROWS:P, G % 4, 2 * j + 1, :],
                                                  ps[ROWS:P, TB, :]).then_inc(t_emptied, 1)
                        if kind == "O":
                            b, g = G // GROUPS, G % GROUPS
                            dve.wait_ge(t_filled, fill_no[kind, j, G] + 1)
                            turned = ps[:, TB, :].rearrange("p (t h d) -> p t h d", t=QT, h=GH)
                            link(nc.vector.reciprocal(rsum[:, :, :], turned[:, :, :, HD]))
                            dst = attn.rearrange("p t (h d) -> p t h d", d=HD)[:, :, GH * g:GH * g + GH, :]
                            for qt in range(QT):
                                o = nc.vector.tensor_tensor(
                                    dst[:, qt], turned[:, qt, :, 0:HD],
                                    rsum[:, qt, :].unsqueeze(2).broadcast_to([P, GH, HD]), ALU.mult)
                            o.then_inc(t_emptied, 1)
                if 0 <= s < NG:
                    shift(s)
                if s == 1:
                    dve.wait_ge(warmed, 1)
                    nc.vector.memset(ps[:, PV, :], 0.0).then_inc(pv_cleared, 1)
                    for p in WO_PIECES:
                        split_high(p)
                b = outproj_at(s)
                for t in range(QT + 1) if b is not None else ():
                    if t < QT:
                        m = b * QT + t
                        dve.wait_ge(at_hi_ready, m + 1)
                        nc.vector.tensor_tensor(at_lo[:, m % 2], ps[:, TB, :].rearrange("p (k n) -> p k n", k=KC),
                                                at_hi[:, m % 2].bitcast(F32), ALU.subtract).then_inc(t_emptied, 1)
                    if t >= 1:
                        u = unit_no["Y", b, t - 1]
                        dve.wait_ge(a_filled, u + 1)
                        x_update(FFN_UPDATES + b * QT + t - 1, u % 2, 1.0)
            norms(2, pieces_at=ffn_pieces(1)[-1])
            ffn(1)

        @block.tensor
        def _(pe):
            def product(dst, w, v, first, last):
                nc.tensor.matmul(dst, w[0], v[0], start=first, stop=False)
                nc.tensor.matmul(dst, w[1], v[0], start=False, stop=False)
                return nc.tensor.matmul(dst, w[0], v[1], start=False, stop=last)

            def turn(phase, t):
                n = phase * TILES + t
                pe.wait_ge(norm_ready, n + 1)
                if n >= 2:
                    pe.wait_ge(xt_ready, n - 1)
                for k in range(KC):
                    last = nc.tensor.transpose(ps[:, turn_bank(phase, t), k * P:(k + 1) * P],
                                               y[:, n % 2, k * P:(k + 1) * P], ident[:, :])
                last.then_inc(norm_turned, 1)

            def unit(f, c, b):
                u = UNITS * f + 2 * c + b
                slot = c % 2
                pe.wait_ge(piece_lo, piece_no["gu", f, c] + 1)
                pe.wait_ge(xt_ready, 2 * TILES * f + 4 * (b + 1))
                if u >= 2:
                    pe.wait_ge(act_f_ready, u - 1)
                at = slice(512 * b, 512 * b + 512)
                for a, bank, done in ((0, u % 2, gate_done), (1, 2 + u % 2, up_done)):
                    for k in range(KC):
                        last = product(ps[:, bank, :], (gu_hi[:, slot, a, k, :], gu_lo[:, slot, a, k, :]),
                                       (xt_hi[:, k, at], xt_lo[:, k, at]), k == 0, k == KC - 1)
                    last.then_inc(done, 1)

            def down(f, r):
                chunks = range(FIRST * r, FIRST * r + FIRST)
                base = updates_before(f) + TILES * r
                pe.wait_ge(piece_lo, piece_no["wd", f, chunks[-1]] + 1)
                for t in range(TILES):
                    pe.wait_ge(act_ready, UNITS * f + 2 * chunks[-1] + t // 4 + 1)
                    if t >= 2:
                        pe.wait_ge(x_updated, base + t - 1)
                    at = slice(t * P, (t + 1) * P)
                    for c in chunks:
                        last = product(ps[:, 4 + t % 2, :], (act_hi[:, c % SLOTS, at], act_lo[:, c % SLOTS, at]),
                                       (wd_hi[:, c % FIRST, :], wd_lo[:, c % FIRST, :]),
                                       c == chunks[0], c == chunks[-1])
                    last.then_inc(down_done, 1)
                    if f == 0 and r == 1 and t >= AHEAD:
                        turn(1, t - AHEAD)

            def ffn(f):
                for c in range(NCH):
                    if c == SLOTS:
                        down(f, 0)
                    for b in range(HALVES):
                        if c == 0:
                            for t in range(4 * b, 4 * b + 4):
                                turn(2 * f, t)
                        unit(f, c, b)
                down(f, 1)

            pe.wait_ge(ident_ready, 1)
            ffn(0)
            for t in range(TILES):
                if t == 0:
                    for ahead in range(TILES - AHEAD, TILES):
                        turn(1, ahead)
                pe.wait_ge(xt_ready, TILES + t + 1)
                pe.wait_ge(piece_lo, piece_no[QK_PIECES[-1]] + 1)
                at = slice(t * P, (t + 1) * P)
                for j in range(3):
                    if t >= 2:
                        if j == 2:
                            pe.wait_ge(qkv_clipped, t - 1)
                        else:
                            pe.wait_ge(q_var_ready, 2 * (t - 2) + j + 1)
                    if j == 2:
                        pe.wait_ge(piece_lo, piece_no[V_PIECES[-1]] + 1)
                    hi, lo, cols = (v_hi, v_lo, slice(0, D)) if j == 2 else (qk_hi, qk_lo, slice(j * D, (j + 1) * D))
                    for k in range(KC):
                        last = product(ps[:, 3 * (t % 2) + j, :], (xt_hi[:, k, at], xt_lo[:, k, at]),
                                       (hi[:, k, cols], lo[:, k, cols]), k == 0, k == KC - 1)
                    last.then_inc(qkv_done, 1)

            def fill(kind, j, G):
                n = fill_no[kind, j, G]
                if kind == "O":
                    pe.wait_ge(o_t_ready, G + 1)
                elif kind == "QB":
                    pe.wait_ge(shift_ready, G + 1)
                else:
                    pe.wait_ge(stack_ready, G + 1)
                if n >= 1:
                    pe.wait_ge(t_emptied, emptied_after[fill_at[n - 1]])
                for t in range(QT):
                    if kind == "O":
                        source = o_t[:, t * P:(t + 1) * P]
                    else:
                        stack = stack_k[:, G % 2, t] if kind == "K" else stack_q[:, G % 3, t]
                        source = stack[:, 2 * j:2 * j + 2, :].rearrange("p h r -> p (h r)")
                        last = nc.tensor.matmul(ps[:, TB, t * P:(t + 1) * P], source, ident_r[:, :],
                                                start=True, stop=True)
                        continue
                    last = nc.tensor.transpose(ps[:, TB, t * P:(t + 1) * P], source, ident[:, :])
                last.then_inc(t_filled, 1)

            def unit_bank_free(m):
                if m >= 2:
                    kind, i, j = unit_at[m - 2]
                    if kind == "A":
                        pe.wait_ge(a_emptied, maxima_taken(i, j))
                    else:
                        pe.wait_ge(x_updated, FFN_UPDATES + QT * i + j + 1)

            def pass_a(G, n):
                m = unit_no["A", G, n]
                qt, heads = a_unit(n)
                width = P * (qt + 1)
                if n == 0:
                    pe.wait_ge(t_emptied, emptied_after["QA", 1, G])
                unit_bank_free(m)
                for e, hh in enumerate(heads):
                    last = nc.tensor.matmul(ps[:, m % 2, e * width:(e + 1) * width],
                                     qa_t[:, G % 2, hh // 2, qt * P:(qt + 1) * P], k_t[:, G % 4, hh, 0:width],
                                     start=(e == 0), stop=True, skip_group_check=True)
                last.then_inc(a_filled, 1)

            def pass_b(G, n):
                idx = B_OPS * G + n
                kc, heads = b_op(n)
                if n == 0:
                    pe.wait_ge(t_emptied, emptied_after["QB", 1, G])
                if idx >= 2:
                    pe.wait_ge(exp_done, idx - 1)
                width = S - kc * P
                for hh, bank, col in heads:
                    nc.tensor.matmul(ps[:, 2 + 2 * (idx % 2) + bank, col:col + width],
                                     k_t[:, G % 4, hh, kc * P:(kc + 1) * P], qb_t[:, G % 2, hh // 2, kc * P:S],
                                     start=(col == 0), stop=False, skip_group_check=True)
                for hh, bank, col in heads:
                    last = nc.tensor.matmul(ps[:, 2 + 2 * (idx % 2) + bank, col:col + P], ident_bf[:, :],
                                            mask_b[:, :], start=False, stop=True, skip_group_check=True)
                last.then_inc(b_filled, 1)

            def probs_v(G, n):
                idx = B_OPS * G + n
                b, g = G // GROUPS, G % GROUPS
                kc, heads = b_op(n)
                if n == 0:
                    pe.wait_ge(pv_cleared, 1)
                    if G >= 1:
                        pe.wait_ge(o_t_ready, G)
                pe.wait_ge(exp_done, idx + 1)
                width = S - kc * P
                for e, (hh, _, _) in enumerate(heads):
                    last = nc.tensor.matmul(ps[32 * hh:32 * hh + VW, PV, kc * P:S], vext[:, b, kc, GH * g + hh, :],
                                            probs[:, idx % 3, e * width:(e + 1) * width],
                                            start=(kc == 0), stop=(kc == QT - 1), skip_group_check=True,
                                            tile_position=(0, 32 * hh))
                last.then_inc(pv_step, 1)

            def keep_warm(n):
                for _ in range(n):
                    last = nc.tensor.matmul(ps[:, PV, :], ident_bf[:, :], mask_a[:, :], start=True, stop=True)
                return last

            pe.wait_ge(masks_ready, 4)
            pe.wait_ge(vones_ready, 1)
            for s in STEPS:
                if s == 0:
                    pe.wait_ge(qk_ready, 2 * TILES)
                    pe.wait_ge(qkv_clipped, TILES)
                for i in range(B_OPS):
                    if s < 2:
                        last = keep_warm(WARM)
                        if (s, i) == (1, B_OPS - 1):
                            last.then_inc(warmed, 1)
                    if 0 <= s - 2 < NG:
                        pass_b(s - 2, i)
                    for n in (2 * i, 2 * i + 1):
                        if 0 <= s < NG and n < A_UNITS:
                            pass_a(s, n)
                    if i >= 1 and 0 <= s - 2 < NG:
                        probs_v(s - 2, i - 1)
                    for kind, j, G in fills_at(s, i):
                        fill(kind, j, G)
                if 0 <= s - 2 < NG:
                    probs_v(s - 2, B_OPS - 1)
                b = outproj_at(s)
                for t in range(QT + 1) if b is not None else ():
                    if t < QT:
                        pe.wait_ge(t_emptied, emptied_after[fill_at[fill_no["AT", b, t] - 1]])
                        for k in range(KC):
                            last = nc.tensor.transpose(ps[:, TB, k * P:(k + 1) * P], attn[:, t, k * P:(k + 1) * P],
                                                       ident[:, :])
                        last.then_inc(t_filled, 1)
                    if t >= 1:
                        m, u = b * QT + t - 1, unit_no["Y", b, t - 1]
                        pe.wait_ge(t_emptied, emptied_after["AT", b, t - 1])
                        pe.wait_ge(piece_lo, piece_no[WO_PIECES[1]] + 1)
                        unit_bank_free(u)
                        for k in range(KC):
                            last = product(ps[:, u % 2, :], (at_hi[:, m % 2, k, :], at_lo[:, m % 2, k, :]),
                                           (wo_hi[:, k, :], wo_lo[:, k, :]), k == 0, k == KC - 1)
                        last.then_inc(a_filled, 1)
            ffn(1)


def contraction_rows():
    slope = (1.0 / np.power(2.0, np.arange(1, H + 1) * (8.0 / H))).astype(np.float32)
    scale = np.exp2(np.floor(np.log2(slope)) - 11).astype(np.float32)
    hi = (np.round(slope / scale) * scale).astype(np.float32)
    lo = slope - hi
    pos = (np.arange(QT)[None, :] * P + np.arange(P)[:, None]).astype(np.float32)[:, :, None]
    rows_q = (hi, -pos, lo, -pos, 0.0, 0.0)
    rows_k = (pos, hi, pos, lo, -1.0, -1.0)
    return [np.ascontiguousarray(np.stack([np.broadcast_to(r, (P, QT, H)) for r in rows], -1), np.float32)
            for rows in (rows_q, rows_k)]


def kernel(L0_attn_hidden_states, L0_attn_w_qkv, L0_attn_q_ln_w, L0_attn_q_ln_b, L0_attn_k_ln_w, L0_attn_k_ln_b,
           L0_attn_w_out, L0_ffn_ln_w, L0_ffn_gate_w, L0_ffn_up_w, L0_ffn_down_w):
    import concourse.bacc as bacc
    from concourse.bass_utils import run_bass_kernel_spmd

    def turned(w, n):
        w = np.asarray(w)
        return w.reshape(w.shape[0] // n, n, KC, P).transpose(0, 3, 2, 1)

    w_gu = np.stack([turned(L0_ffn_gate_w, P), turned(L0_ffn_up_w, P)], 2)
    con_q, con_k = contraction_rows()
    arrays = {
        "x_in": np.asarray(L0_attn_hidden_states).reshape(B * S, D),
        "w_gu": w_gu.reshape(NCH, P, PIECE),
        "w_down": np.asarray(L0_ffn_down_w).T.reshape(NCH, P, D),
        "w_qkv": turned(L0_attn_w_qkv, 256).reshape(6, P, PIECE),
        "w_out": turned(L0_attn_w_out, 256).reshape(2, P, PIECE),
        "ln_w": np.asarray(L0_ffn_ln_w).reshape(1, D),
        "q_w": np.asarray(L0_attn_q_ln_w).reshape(1, D),
        "q_b": np.asarray(L0_attn_q_ln_b).reshape(1, D),
        "k_w": np.asarray(L0_attn_k_ln_w).reshape(1, D),
        "k_b": np.asarray(L0_attn_k_ln_b).reshape(1, D),
        "con_q": con_q,
        "con_k": con_k,
    }
    arrays = {name: np.ascontiguousarray(a) for name, a in arrays.items()}
    nc = bacc.Bacc("TRN2", target_bir_lowering=False, num_devices=1)
    ins = [nc.dram_tensor(name, a.shape, F32, kind="ExternalInput").ap() for name, a in arrays.items()]
    out = nc.dram_tensor("out", (B * S, D), F32, kind="ExternalOutput").ap()
    build(nc, *ins, out)
    got = run_bass_kernel_spmd(nc, [arrays], core_ids=[0])
    return got.results[0]["out"].reshape(B, S, D)
```

```python
from contextlib import ExitStack

import numpy as np

import concourse.bass as bass
from concourse import mybir

ALU = mybir.AluOpType
ACT = mybir.ActivationFunctionType
F32 = mybir.dt.float32
F32R = mybir.dt.float32r
BF16 = mybir.dt.bfloat16

P = 128
B, S, D = 2, 512, 512
I = 1792
H = 32
HD = D // H
KC = D // P
TILES = B * S // P
NCH = I // P
FIRST = 7
AHEAD = 2
SLOTS = FIRST + 1
HALVES = B * S // 512
UNITS = NCH * HALVES
EPS = 1e-5
CLIP = 8.0
MASKED = -3.0e38

RAW = 3
PIECE = KC * 2 * P

GH = 4
GROUPS = H // GH
NG = B * GROUPS
QT = S // P
ROWS = 64
CON = 6
A_UNITS = 12
B_OPS = 6
WARM = 2
YS = 3
FIRST_HIGH = (0, 4, 5)
FIRST_LOW = ((2, 4, 5), (3, 3, 7))
NS = 4
VW = HD + 1


QK_PIECES = [("qk", 0, j) for j in range(4)]
V_PIECES = [("v", 0, j) for j in range(2)]
QKV_PIECES = QK_PIECES + V_PIECES
WO_PIECES = [("wo", 0, j) for j in range(2)]


def ffn_pieces(f):
    def gu(c):
        return ("gu", f, c)

    def wd(c):
        return ("wd", f, c)

    after = {-1: [gu(0), gu(1), wd(0)]}
    for c in range(5):
        after[c] = [gu(c + 2), wd(c + 1)]
    after[5] = [gu(7), wd(6)]
    after[6] = [gu(8)]
    after[7] = [gu(9)]
    after[8] = [gu(10), wd(7), wd(8)]
    after[9] = [gu(11), wd(9)]
    after[10] = [gu(12), wd(10)]
    after[11] = [gu(13), wd(11)]
    after[12] = [wd(12), wd(13)]
    after[13] = []
    return after


UNIT_ORDER = [(0, 0), (1, 0), (0, 1), (1, 1)] + [(c, b) for c in range(2, NCH) for b in range(HALVES)]


def units_through(c):
    return UNIT_ORDER.index((c, HALVES - 1)) + 1


def slot_of(c):
    return (c + 1) % SLOTS


def fills_at(s, i):
    kind, j = [("QB", 0), ("K", 0), ("QB", 1), ("K", 1), ("QA", 0), ("QA", 1)][i]
    G = s - 1 if kind == "QB" else s + 1
    return [(kind, j, G)] if 0 <= G < NG else []


OUTPROJ_STEP = GROUPS - 1 + 3

TURNS_AT = {(NG, 4): 0, (NG, 5): 1, (NG + 1, 1): 2, (NG + 1, 2): 3}
LOWS_AT = {(NG, 5): 0, (NG + 1, 1): 1, (NG + 1, 2): 2, (NG + 1, 3): 3}


PV_AT = {2: (0, 1), 4: (2, 3), 5: (4,)}

STEPS = range(-1, NG + 2)


def number_attention():
    fills, units = {}, {}
    for s in STEPS:
        for i in range(B_OPS):
            for n in (2 * i, 2 * i + 1):
                if 0 <= s < NG and n < A_UNITS:
                    units[("A", s, n)] = len(units)
            for f in fills_at(s, i):
                fills[f] = len(fills)
        if s == OUTPROJ_STEP:
            for t in range(QT):
                fills["AT", 0, t] = len(fills)
                units["Y", 0, t] = len(units)
    for t in range(QT):
        fills["AT", 1, t] = len(fills)
        units["Y", 1, t] = len(units)
    return fills, units


def a_unit(n):
    if n < 4:
        return n % 2, [2 * (n // 2), 2 * (n // 2) + 1]
    return 2 + (n - 4) // GH, [(n - 4) % GH]


def maxima_taken(G, n):
    return GH * QT * G + (2 * (n + 1) if n < 4 else n + 5)


def b_op(n):
    if n < 4:
        kc, first = n // 2, 2 * (n % 2)
        return kc, [(first, 0, 0), (first + 1, 1, 0)]
    kc = n - 2
    return kc, [(hh, hh % 2, (S - kc * P) * (hh // 2)) for hh in (0, 2, 1, 3)]


def build(nc, x_in, w_gu, w_down, w_qkv, w_out, ln_w, q_w, q_b, k_w, k_b, con_q, con_k, out):
    persistent = ExitStack()
    with persistent:
        def sem(name):
            return persistent.enter_context(nc.semaphore(name))

        def allocate(stack, name, shape, dt):
            return stack.enter_context(nc.sbuf_tensor(name, shape, dt))

        def sb(name, shape, dt=F32):
            return allocate(persistent, name, shape, dt)

        x = sb("x", [P, TILES, D])
        raw = sb("raw", [P, RAW, PIECE])
        lnw_row = sb("lnw_row", [P, D])
        ident = sb("ident", [P, P])
        ident_bf = sb("ident_bf", [P, P], BF16)
        mask = sb("mask", [P, S], BF16)
        y = sb("y", [P, YS, D])
        ident_r = sb("ident_r", [P, P], F32R)
        stats = sb("stats", [P, NS, 6])
        mean_var = sb("mean_var", [P, NS, 2])
        power = sb("power", [P, 1])
        rstd = sb("rstd", [P, NS, 1])
        q_stats = sb("q_stats", [P, 2, 6])
        q_mean_var = sb("q_mean_var", [P, 4, 2])
        q_rstd = sb("q_rstd", [P, 4, 1])
        row_max = sb("row_max", [P, 2, QT, GH])
        rsum = sb("rsum", [P, QT, GH])

        far = ExitStack()
        xt_hi = far.enter_context(nc.sbuf_tensor("xt_hi", [P, KC, B * S], F32R, side="right"))
        xt_lo = far.enter_context(nc.sbuf_tensor("xt_lo", [P, KC, B * S], F32R, side="right"))
        qk_hi = far.enter_context(nc.sbuf_tensor("qk_hi", [P, KC, 2 * D], F32R, side="right"))
        qk_lo = far.enter_context(nc.sbuf_tensor("qk_lo", [P, KC, 2 * D], F32R, side="right"))
        v_hi = far.enter_context(nc.sbuf_tensor("v_hi", [P, KC, D], F32R, side="right"))
        v_lo = far.enter_context(nc.sbuf_tensor("v_lo", [P, KC, D], F32R, side="right"))
        far.close()

        with ExitStack() as ffn_stage:
            wd_hi = allocate(ffn_stage, "wd_hi", [P, FIRST, D], F32R)
            wd_lo = allocate(ffn_stage, "wd_lo", [P, FIRST, D], F32R)
            act_hi = allocate(ffn_stage, "act_hi", [P, SLOTS, B * S], F32R)
            act_lo = allocate(ffn_stage, "act_lo", [P, SLOTS, B * S], F32R)
            gu_hi = allocate(ffn_stage, "gu_hi", [P, 2, 2, KC, P], F32R)
            gu_lo = allocate(ffn_stage, "gu_lo", [P, 2, 2, KC, P], F32R)
            silu_g = allocate(ffn_stage, "silu_g", [P, 2, 512], F32)
            act_f = allocate(ffn_stage, "act_f", [P, 2, 512], F32)
        memory = [(xt_hi, xt_lo, wd_hi, wd_lo, act_hi, act_lo, gu_hi, gu_lo, silu_g, act_f)]

        mid = ExitStack()
        qn = allocate(mid, "qn", [P, B, QT, D], F32)
        kn = allocate(mid, "kn", [P, B, QT, D], F32)
        stack_k = allocate(mid, "stack_k", [P, 2, QT, GH, ROWS], F32R)
        stack_q = allocate(mid, "stack_q", [P, 3, QT, GH, ROWS], F32R)
        cq = allocate(mid, "cq", [P, QT, H, CON], F32)
        ck = allocate(mid, "ck", [P, QT, H, CON], F32)
        vext = allocate(mid, "vext", [P, B, QT, H, VW], F32)
        with ExitStack() as qkv_stage:
            wb = allocate(qkv_stage, "wb", [P, 4, D], F32)

        with ExitStack() as att:
            attn = allocate(att, "attn", [P, QT, D], F32)
            at_hi = allocate(att, "at_hi", [P, 2, KC, P], F32R)
            at_lo = allocate(att, "at_lo", [P, 2, KC, P], F32R)
            probs = allocate(att, "probs", [P, 3, 1024], F32)
            k_t = allocate(att, "k_t", [P, 4, GH, S], F32R)
            qa_t = allocate(att, "qa_t", [P, 2, 2, S], F32R)
            qb_t = allocate(att, "qb_t", [P, 2, 2, S], F32R)
            wo_hi = allocate(att, "wo_hi", [P, KC, D], F32R)
            wo_lo = allocate(att, "wo_lo", [P, KC, D], F32R)
            o_t = allocate(att, "o_t", [P, S], F32)
        mid.close()

        with ExitStack() as last:
            xt_hi2 = allocate(last, "xt_hi2", [P, KC, B * S], F32R)
            xt_lo2 = allocate(last, "xt_lo2", [P, KC, B * S], F32R)
            gu_hi2 = allocate(last, "gu_hi2", [P, 2, 2, KC, P], F32R)
            gu_lo2 = allocate(last, "gu_lo2", [P, 2, 2, KC, P], F32R)
            silu_g2 = allocate(last, "silu_g2", [P, 2, 512], F32)
            act_f2 = allocate(last, "act_f2", [P, 2, 512], F32)
            act_hi2 = allocate(last, "act_hi2", [P, SLOTS, B * S], F32R)
            act_lo2 = allocate(last, "act_lo2", [P, SLOTS, B * S], F32R)
            wd_hi2 = allocate(last, "wd_hi2", [P, FIRST, D], F32R)
            wd_lo2 = allocate(last, "wd_lo2", [P, FIRST, D], F32R)
        memory += [(xt_hi2, xt_lo2, wd_hi2, wd_lo2, act_hi2, act_lo2, gu_hi2, gu_lo2, silu_g2, act_f2)]
        xt_his, xt_los, wd_his, wd_los, act_his, act_los, gu_his, gu_los, silu_gs, act_fs = zip(*memory)

        ps = persistent.enter_context(nc.psum_tensor("ps", [P, 8, 512], F32))
        PV, TB = 6, 7

        x_loaded = [sem(f"x_loaded{t}") for t in range(TILES)]
        lnw_loaded = sem("lnw_loaded")
        stats_ready = sem("stats_ready")
        y_centred = sem("y_centred")
        cons_loaded = sem("cons_loaded")
        wb_loaded = sem("wb_loaded")
        warmed = sem("warmed")
        k_zeroed = sem("k_zeroed")
        raw_loaded = [sem(f"raw_loaded{n}") for n in range(RAW)]
        piece_hi = sem("piece_hi")
        piece_lo = sem("piece_lo")
        ident_ready = sem("ident_ready")
        masks_ready = sem("masks_ready")
        dve_step = sem("dve_step")
        pool_step = sem("pool_step")
        var_ready = sem("var_ready")
        rstd_ready = sem("rstd_ready")
        norm_ready = sem("norm_ready")
        norm_turned = sem("norm_turned")
        xt_hi_ready = sem("xt_hi_ready")
        xt_ready = sem("xt_ready")
        gate_done = sem("gate_done")
        up_done = sem("up_done")
        silu_done = sem("silu_done")
        act_f_ready = sem("act_f_ready")
        act_hi_ready = sem("act_hi_ready")
        act_ready = sem("act_ready")
        down_done = sem("down_done")
        x_updated = sem("x_updated")
        qkv_done = sem("qkv_done")
        qkv_clipped = sem("qkv_clipped")
        q_var_ready = sem("q_var_ready")
        q_rstd_ready = sem("q_rstd_ready")
        qk_ready = sem("qk_ready")
        vones_ready = sem("vones_ready")
        stack_ready = sem("stack_ready")
        pv_cleared = sem("pv_cleared")
        t_filled = sem("t_filled")
        t_emptied = sem("t_emptied")
        a_filled = sem("a_filled")
        a_emptied = sem("a_emptied")
        shift_ready = sem("shift_ready")
        b_filled = sem("b_filled")
        exp_done = sem("exp_done")
        pv_step = sem("pv_step")
        o_t_ready = sem("o_t_ready")
        o_turned = sem("o_turned")
        o_taken = sem("o_taken")
        at_hi_ready = sem("at_hi_ready")
        stored = sem("stored")

        pieces = []
        for f in range(2):
            after = ffn_pieces(f)
            pieces += [p for c in range(-1, NCH) for p in after[c]]
            if f == 0:
                pieces += QKV_PIECES + WO_PIECES
        piece_no = {p: n for n, p in enumerate(pieces)}
        fill_no, unit_no = number_attention()
        unit_at = {n: unit for unit, n in unit_no.items()}
        fill_at = {n: fill for fill, n in fill_no.items()}
        emptied_after, count = {}, 0
        for fill in fill_no:
            count += 2 if fill[0] == "K" else 1
            emptied_after[fill] = count
        FFN_UPDATES = 2 * TILES
        ATT_UPDATES = TILES

        def updates_before(f):
            return f * (FFN_UPDATES + ATT_UPDATES)

        def turn_bank(phase, t):
            if phase == 0:
                return 4 + t % 4
            return t % 2 if phase == 2 and t < TILES // 2 else 6 + t % 2

        def fill_bank(kind, j, G):
            return {("K", 1, 0): 6, ("QA", 0, 0): 2, ("QA", 1, 0): 1}.get((kind, j, G), TB)

        def projection_bank(b, t):
            return unit_no["Y", b, t] % 2 if b == 0 else 4 + t % 2

        def piece_source(p):
            kind, _, c = p
            if kind == "gu":
                return w_gu[c], PIECE
            if kind == "wd":
                return w_down[c], D
            return {"qk": w_qkv[c], "v": w_qkv[4 + c % 2], "wo": w_out[c % 2]}[kind], PIECE

        def piece_views(p):
            kind, f, c = p
            slot = raw[:, piece_no[p] % RAW, :]
            if kind == "gu":
                v = slot.rearrange("p (a k n) -> p a k n", a=2, k=KC)
                return v, gu_his[f][:, c % 2], gu_los[f][:, c % 2]
            if kind == "wd":
                return slot[:, 0:D], wd_his[f][:, c % FIRST, :], wd_los[f][:, c % FIRST, :]
            v = slot.rearrange("p (k n) -> p k n", k=KC)
            hi, lo = {"qk": (qk_hi, qk_lo), "v": (v_hi, v_lo), "wo": (wo_hi, wo_lo)}[kind]
            return v, hi[:, :, 256 * c:256 * c + 256], lo[:, :, 256 * c:256 * c + 256]

        block = persistent.enter_context(nc.Block())

        @block.sync
        def _(sp):
            for t in range(TILES):
                sp.dma_start(x[:, t, :], x_in[t * P:(t + 1) * P, :]).then_inc(x_loaded[t], 16)
                if t == 0:
                    sp.dma_start(lnw_row[:, :], ln_w.broadcast_to([P, D])).then_inc(lnw_loaded, 16)
                if 1 <= t <= RAW:
                    source, n = piece_source(pieces[t - 1])
                    sp.dma_start(raw[:, t - 1, 0:n], source).then_inc(raw_loaded[t - 1], 16)
            for n, p in enumerate(pieces):
                if n < RAW:
                    continue
                if p == WO_PIECES[1]:
                    sp.wait_ge(x_updated, FFN_UPDATES)
                    for j, row in enumerate((q_w, q_b, k_w, k_b)):
                        sp.dma_start(wb[:, j, :], row.broadcast_to([P, D])).then_inc(wb_loaded, 16)
                    sp.dma_start(cq[:, :, :, :], con_q).then_inc(cons_loaded, 16)
                    sp.dma_start(ck[:, :, :, :], con_k).then_inc(cons_loaded, 16)
                sp.wait_ge(piece_lo, n - RAW + 1)
                source, size = piece_source(p)
                sp.dma_start(raw[:, n % RAW, 0:size], source).then_inc(raw_loaded[n % RAW], 16)
            base = updates_before(1) + TILES
            for t in range(TILES):
                sp.wait_ge(x_updated, base + t + 1)
                sp.dma_start(out[t * P:(t + 1) * P, :], x[:, t, :]).then_inc(stored, 16)
            sp.wait_ge(stored, 16 * TILES)

        @block.gpsimd
        def _(pool):
            steps = [0]

            def link(ins):
                steps[0] += 1
                ins.then_inc(pool_step, 1)
                pool.wait_ge(pool_step, steps[0])

            link(nc.gpsimd.memset(ident[:, :], 0.0))
            link(nc.gpsimd.affine_select(out=ident[:, :], in_=ident[:, :], compare_op=ALU.not_equal, fill=1.0,
                                         base=0, pattern=[[-1, P]], channel_multiplier=1))
            nc.gpsimd.memset(power[:, :], -0.5).then_inc(ident_ready, 1)
            pool.wait_ge(ident_ready, 1)

            nc.gpsimd.tensor_copy(ident_bf[:, :], ident[:, :]).then_inc(masks_ready, 1)
            nc.gpsimd.tensor_copy(ident_r[:, :], ident[:, :]).then_inc(masks_ready, 1)
            link(nc.gpsimd.memset(mask[:, :], 0.0))
            nc.gpsimd.affine_select(out=mask[:, :], in_=mask[:, :], compare_op=ALU.is_ge, fill=MASKED,
                                    base=S - P, pattern=[[-1, S]], channel_multiplier=1).then_inc(masks_ready, 1)

            def inverse_root(dst, src, scale, eps):
                link(nc.gpsimd.tensor_scalar(dst, src, scale, eps, ALU.mult, ALU.add))
                return nc.gpsimd.tensor_tensor(dst, dst, power[:, :], ALU.pow)

            def norm_tile(phase, t):
                n = phase * TILES + t
                r, var = rstd[:, n % NS, :], mean_var[:, n % NS, 1:2]
                pool.wait_ge(var_ready, n + 1)
                if phase == 1:
                    inverse_root(r, var, 1.0, EPS).then_inc(rstd_ready, 1)
                else:
                    inverse_root(r, var, 1.0 + EPS, EPS * EPS).then_inc(rstd_ready, 1)

            def split_low(p):
                v, hi, lo = piece_views(p)
                pool.wait_ge(piece_hi, piece_no[p] + 1)
                nc.gpsimd.tensor_tensor(lo, v, hi.bitcast(F32), ALU.subtract).then_inc(piece_lo, 1)

            def norm_half(f, b):
                for t in range(4 * b, 4 * b + 4):
                    norm_tile(2 * f, t)
                    for p, at in zip(ffn_pieces(f)[-1], FIRST_LOW[f]):
                        if t == at:
                            split_low(p)

            def low(f, u):
                c, b = UNIT_ORDER[u]
                n = UNITS * f + u
                pool.wait_ge(act_hi_ready, n + 1)
                at = slice(512 * b, 512 * b + 512)
                nc.gpsimd.tensor_tensor(act_los[f][:, slot_of(c), at], act_fs[f][:, n % 2, :],
                                        act_his[f][:, slot_of(c), at].bitcast(F32),
                                        ALU.subtract).then_inc(act_ready, 1)

            def ffn(f, first):
                for u in range(first, UNITS):
                    c, b = UNIT_ORDER[u]
                    after = ffn_pieces(f)[c] if b == HALVES - 1 else []
                    for p in after[:1]:
                        split_low(p)
                    low(f, u)
                    for p in after[1:]:
                        split_low(p)

            def stack(G, i):
                b, g = G // GROUPS, G % GROUPS
                sk, sq = stack_k[:, G % 2], stack_q[:, G % 3]
                heads = slice(GH * g, GH * g + GH)
                q = qn[:, b].rearrange("p t (h d) -> p t h d", d=HD)[:, :, heads, :]
                k = kn[:, b].rearrange("p t (h d) -> p t h d", d=HD)[:, :, heads, :]
                if i == 0:
                    if G == 0:
                        pool.wait_ge(cons_loaded, 16 * 2)
                    pool.wait_ge(qk_ready, TILES * (b + 1))
                    if G >= 2:
                        pool.wait_ge(t_filled, fill_no["K", 1, G - 2] + 1)
                    nc.gpsimd.tensor_copy(sk[:, :, :, 16:32], k)
                    nc.gpsimd.tensor_copy(sk[:, :, :, 0:CON], ck[:, :, heads, :])
                elif i == 1:
                    link(nc.gpsimd.tensor_copy(sk[:, :, :, 32:48], k))
                elif i == 2:
                    nc.gpsimd.tensor_tensor(sk[:, :, :, 48:64], k, sk[:, :, :, 32:48].bitcast(F32), ALU.subtract)
                elif i == 3:
                    if G >= 3:
                        pool.wait_ge(t_filled, fill_no["QB", 1, G - 3] + 1)
                    nc.gpsimd.tensor_copy(sq[:, :, :, 16:32], q)
                    nc.gpsimd.tensor_copy(sq[:, :, :, 0:CON], cq[:, :, heads, :])
                elif i == 4:
                    link(nc.gpsimd.tensor_copy(sq[:, :, :, 48:64], q))
                else:
                    nc.gpsimd.tensor_tensor(sq[:, :, :, 32:48], q, sq[:, :, :, 48:64].bitcast(F32),
                                            ALU.subtract).then_inc(stack_ready, 1)

            norm_half(0, 0)
            norm_half(0, 1)
            ffn(0, 0)
            for t in range(TILES):
                norm_tile(1, t)
                if t < len(QKV_PIECES):
                    split_low(QKV_PIECES[t])
            pool.wait_ge(x_updated, FFN_UPDATES)
            link(nc.gpsimd.memset(stack_k[:, :, :, :, :].bitcast(F32), 0.0))
            link(nc.gpsimd.memset(stack_q[:, :, :, :, :].bitcast(F32), 0.0))
            for n in range(2 * TILES):
                pool.wait_ge(q_var_ready, n + 1)
                inverse_root(q_rstd[:, n % 4, :], q_mean_var[:, n % 4, 1:2], 1.0, EPS).then_inc(q_rstd_ready, 1)
                if n in (11, 13):
                    for i in range(B_OPS):
                        stack(n // 2 - 5, i)
            pool.wait_ge(qkv_done, 3 * TILES)
            for n in range(4):
                for j in range(2):
                    nc.gpsimd.memset(k_t[:, n, 2 * j:2 * j + 2, :].bitcast(F32), 0.0).then_inc(k_zeroed, 1)
            for s in STEPS:
                for i in range(B_OPS):
                    if 2 <= s + 2 < NG:
                        stack(s + 2, i)
                if s == 1:
                    for p in WO_PIECES:
                        split_low(p)
            norm_half(1, 0)
            low(1, 0)
            norm_half(1, 1)
            ffn(1, 1)

        @block.scalar
        def _(act):
            def turn_high(phase, t):
                n = phase * TILES + t
                act.wait_ge(norm_turned, n + 1)
                nc.scalar.activation(xt_his[phase // 2][:, :, t * P:(t + 1) * P],
                                     ps[:, turn_bank(phase, t), :].rearrange("p (k n) -> p k n", k=KC),
                                     ACT.Copy).then_inc(xt_hi_ready, 1)

            def split_high(p):
                n = piece_no[p]
                v, hi, _ = piece_views(p)
                act.wait_ge(raw_loaded[n % RAW], 16 * (n // RAW + 1))
                nc.scalar.activation(hi, v, ACT.Copy).then_inc(piece_hi, 1)

            def scale_tile(f, t):
                n = 2 * f * TILES + t
                act.wait_ge(y_centred, TILES * f + t + 1)
                act.wait_ge(rstd_ready, n + 1)
                nc.scalar.activation(y[:, n % YS, :], y[:, n % YS, :], ACT.Copy,
                                     scale=rstd[:, n % NS, :]).then_inc(norm_ready, 1)

            def silu(f, u):
                n = UNITS * f + u
                act.wait_ge(gate_done, n + 1)
                if n >= 2:
                    act.wait_ge(act_f_ready, n - 1)
                nc.scalar.activation(silu_gs[f][:, n % 2, :], ps[:, n % 2, :], ACT.Silu).then_inc(silu_done, 1)

            def high(f, u):
                c, b = UNIT_ORDER[u]
                n = UNITS * f + u
                act.wait_ge(act_f_ready, n + 1)
                if c >= SLOTS:
                    act.wait_ge(down_done, FFN_UPDATES * f + TILES)
                nc.scalar.activation(act_his[f][:, slot_of(c), 512 * b:512 * b + 512], act_fs[f][:, n % 2, :],
                                     ACT.Copy).then_inc(act_hi_ready, 1)

            def ffn(f, first):
                for u in range(first, UNITS):
                    if (f, u) != (0, 0):
                        silu(f, u)
                    if u > first:
                        high(f, u - 1)
                high(f, UNITS - 1)

            first_pieces = ffn_pieces(0)[-1]
            for t in range(TILES + 1):
                if t < TILES:
                    scale_tile(0, t)
                if t >= 1:
                    turn_high(0, t - 1)
                if t in FIRST_HIGH:
                    split_high(first_pieces[FIRST_HIGH.index(t)])
                if t == TILES - 1:
                    silu(0, 0)
            ffn(0, 0)
            for t in range(TILES):
                turn_high(1, t)

            def exp(G, n):
                idx = B_OPS * G + n
                kc, heads = b_op(n)
                bank = 2 + 2 * (idx % 2)
                act.wait_ge(b_filled, idx + 1)
                if idx >= 3:
                    act.wait_ge(pv_step, idx - 2)
                width = (S - kc * P) * len(heads) // 2
                nc.scalar.activation(probs[:, idx % 3, 0:2 * width].rearrange("p (a n) -> p a n", a=2),
                                     ps[:, bank:bank + 2, 0:width], ACT.Exp).then_inc(exp_done, 1)

            def evacuate(kind, j, G):
                n = fill_no[kind, j, G]
                act.wait_ge(t_filled, n + 1)
                if kind == "K":
                    if G < 4:
                        act.wait_ge(k_zeroed, 2 * G + j + 1)
                    nc.scalar.activation(k_t[0:ROWS, G % 4, 2 * j, :], ps[0:ROWS, fill_bank(kind, j, G), :],
                                         ACT.Copy).then_inc(t_emptied, 1)
                else:
                    dst = {"QA": qa_t, "QB": qb_t}[kind][:, G % 2, j, :]
                    nc.scalar.activation(dst, ps[:, fill_bank(kind, j, G), :], ACT.Copy).then_inc(t_emptied, 1)

            def attn_high(b, t):
                m = b * QT + t
                act.wait_ge(t_filled, fill_no["AT", b, t] + 1)
                if m >= 2:
                    act.wait_ge(a_filled, unit_no["Y", (m - 2) // QT, (m - 2) % QT] + 1)
                nc.scalar.activation(at_hi[:, m % 2], ps[:, TB, :].rearrange("p (k n) -> p k n", k=KC),
                                     ACT.Copy).then_inc(at_hi_ready, 1)

            next_pieces = ffn_pieces(1)[-1]
            for s in STEPS:
                for i in range(B_OPS):
                    if 0 <= s - 2 < NG:
                        exp(s - 2, i)
                    for kind, j, G in fills_at(s, i):
                        evacuate(kind, j, G)
                    if (s, i) == (NG, 3):
                        act.wait_ge(stack_ready, NG)
                        scale_tile(1, 0)
                    if (s, i) in TURNS_AT:
                        t = TURNS_AT[s, i]
                        if t < 3:
                            scale_tile(1, t + 1)
                        turn_high(2, t)
                    if (s, i) in ((NG + 1, 2), (NG + 1, 3)):
                        split_high(next_pieces[i - 2])
                if 0 <= s - 2 < NG:
                    G = s - 2
                    act.wait_ge(pv_step, B_OPS * G + B_OPS)
                    if G >= 1:
                        act.wait_ge(o_turned, G)
                    nc.scalar.activation(o_t[:, :], ps[:, PV, :], ACT.Copy).then_inc(o_t_ready, 1)
                if s == OUTPROJ_STEP:
                    for t in range(QT):
                        attn_high(0, t)

            attn_high(1, 0)
            silu(1, 0)
            attn_high(1, 1)
            high(1, 0)
            attn_high(1, 2)
            scale_tile(1, 4)
            attn_high(1, 3)
            scale_tile(1, 5)
            scale_tile(1, 6)
            for t in range(4, TILES):
                turn_high(2, t)
                if t == 4:
                    scale_tile(1, 7)
            split_high(next_pieces[2])
            ffn(1, 1)

        @block.vector
        def _(dve):
            steps = [0]

            def link(ins):
                steps[0] += 1
                ins.then_inc(dve_step, 1)
                dve.wait_ge(dve_step, steps[0])

            def norm_stats(phase, t):
                n = phase * TILES + t
                if phase == 0:
                    dve.wait_ge(x_loaded[t], 16)
                else:
                    dve.wait_ge(x_updated, (FFN_UPDATES if phase == 1 else updates_before(1)) - TILES + t + 1)
                if n >= NS:
                    dve.wait_ge(rstd_ready, n - NS + 1)
                nc.vector.bn_stats(stats[:, n % NS, :], x[:, t, :]).then_inc(stats_ready, 1)

            def norm_moments(phase, t):
                n = phase * TILES + t
                dve.wait_ge(stats_ready, n + 1)
                nc.vector.bn_aggr(mean_var[:, n % NS, :], stats[:, n % NS, :]).then_inc(var_ready, 1)

            def norm_apply(phase, t):
                n = phase * TILES + t
                if phase == 1:
                    dve.wait_ge(rstd_ready, n + 1)
                dve.wait_ge(var_ready, n + 1)
                if n >= YS:
                    dve.wait_ge(norm_turned, n - YS + 1)
                if phase == 1:
                    nc.vector.tensor_scalar(y[:, n % YS, :], x[:, t, :], mean_var[:, n % NS, 0:1],
                                            rstd[:, n % NS, :], ALU.subtract, ALU.mult).then_inc(norm_ready, 1)
                else:
                    if phase == 0 and t == 0:
                        dve.wait_ge(lnw_loaded, 16)
                    nc.vector.scalar_tensor_tensor(out=y[:, n % YS, :], in0=x[:, t, :], scalar=mean_var[:, n % NS, 0:1],
                                                   in1=lnw_row[:, :], op0=ALU.subtract,
                                                   op1=ALU.mult).then_inc(y_centred, 1)

            def turn_low(phase, t):
                n = phase * TILES + t
                at = slice(t * P, (t + 1) * P)
                dve.wait_ge(xt_hi_ready, n + 1)
                xt_hi, xt_lo = xt_his[phase // 2], xt_los[phase // 2]
                nc.vector.tensor_tensor(xt_lo[:, :, at], ps[:, turn_bank(phase, t), :].rearrange("p (k n) -> p k n", k=KC),
                                        xt_hi[:, :, at].bitcast(F32), ALU.subtract).then_inc(xt_ready, 1)

            def split_high(p):
                kind, f, c = p
                n = piece_no[p]
                v, hi, _ = piece_views(p)
                dve.wait_ge(raw_loaded[n % RAW], 16 * (n // RAW + 1))
                if kind == "gu" and c >= 2:
                    dve.wait_ge(up_done, UNITS * f + units_through(c - 2))
                if kind == "wd" and c >= FIRST:
                    dve.wait_ge(down_done, FFN_UPDATES * f + TILES)
                nc.vector.tensor_copy(hi, v).then_inc(piece_hi, 1)

            def norms(phase, before=None, pieces_after=()):
                lag = 2 if phase == 1 else 3
                for t in range(TILES + lag):
                    if t < TILES:
                        if before:
                            before(t)
                        norm_stats(phase, t)
                    if (phase, t - lag) == (0, TILES - 1):
                        gated(0, 0)
                    if t >= lag:
                        turn_low(phase, t - lag)
                    if t < TILES:
                        norm_moments(phase, t)
                    if phase != 1:
                        if t < TILES:
                            norm_apply(phase, t)
                    elif 1 <= t <= TILES:
                        norm_apply(phase, t - 1)
                    if t < len(pieces_after):
                        split_high(pieces_after[t])

            def x_update(n, bank, scale):
                t = n % TILES
                if n >= TILES:
                    dve.wait_ge(x_updated, n - TILES + 1)
                nc.vector.scalar_tensor_tensor(out=x[:, t, :], in0=ps[:, bank, :], scalar=scale, in1=x[:, t, :],
                                               op0=ALU.mult, op1=ALU.add).then_inc(x_updated, 1)

            def gated(f, u):
                n = UNITS * f + u
                dve.wait_ge(silu_done, n + 1)
                dve.wait_ge(up_done, n + 1)
                if n >= 2:
                    dve.wait_ge(act_ready, n - 1)
                nc.vector.tensor_tensor(act_fs[f][:, n % 2, :], ps[:, 2 + n % 2, :], silu_gs[f][:, n % 2, :],
                                        ALU.mult).then_inc(act_f_ready, 1)

            def out_tile(f, r, t):
                dve.wait_ge(down_done, FFN_UPDATES * f + TILES * r + t + 1)
                x_update(updates_before(f) + TILES * r + t, 4 + t % 2, 0.5)

            def ffn(f, first):
                for u in range(first, UNITS):
                    c, b = UNIT_ORDER[u]
                    if (c, b) == (SLOTS, 0):
                        for t in range(TILES):
                            out_tile(f, 0, t)
                    gated(f, u)
                    if b == HALVES - 1:
                        for p in ffn_pieces(f)[c]:
                            split_high(p)

            norms(0)
            ffn(0, 1)
            dve.wait_ge(act_ready, UNITS)
            norms(1, before=lambda t: out_tile(0, 1, t), pieces_after=QKV_PIECES)
            dve.wait_ge(x_updated, FFN_UPDATES)
            nc.vector.memset(vext[:, :, :, :, HD:VW], 1.0).then_inc(vones_ready, 1)
            dve.wait_ge(wb_loaded, 16 * 4)
            link(nc.vector.tensor_scalar(wb[:, 0:2, :], wb[:, 0:2, :], float(HD) ** -0.5, None, ALU.mult))
            for t in range(TILES):
                for j in range(2):
                    n = 2 * t + j
                    qc = y[:, (2 * TILES + n) % YS, :]
                    if n < YS:
                        dve.wait_ge(norm_turned, 2 * TILES + n - YS + 1)
                    dve.wait_ge(qkv_done, 3 * t + j + 1)
                    link(nc.vector.tensor_scalar(qc, ps[:, 3 * (t % 2) + j, :], CLIP, -CLIP,
                                                 ALU.min, ALU.max))
                    link(nc.vector.bn_stats(q_stats[:, j, :], qc))
                    link(nc.vector.bn_aggr(q_mean_var[:, n % 4, :], q_stats[:, j, :]))
                    nc.vector.scalar_tensor_tensor(out=qc, in0=qc,
                                                   scalar=q_mean_var[:, n % 4, 0:1], in1=wb[:, 2 * j, :],
                                                   op0=ALU.subtract, op1=ALU.mult).then_inc(q_var_ready, 1)
                dve.wait_ge(qkv_done, 3 * t + 3)
                nc.vector.tensor_scalar(vext[:, t // QT, t % QT, :, 0:HD],
                                        ps[:, 3 * (t % 2) + 2, :].rearrange("p (h d) -> p h d", d=HD),
                                        CLIP, -CLIP, ALU.min, ALU.max).then_inc(qkv_clipped, 1)
                for j in range(2):
                    n = 2 * t + j
                    qc = y[:, (2 * TILES + n) % YS, :]
                    dve.wait_ge(q_rstd_ready, n + 1)
                    dve.wait_ge(q_var_ready, n + 1)
                    nc.vector.scalar_tensor_tensor(out=(qn, kn)[j][:, t // QT, t % QT, :], in0=qc,
                                                   scalar=q_rstd[:, n % 4, :], in1=wb[:, 2 * j + 1, :],
                                                   op0=ALU.mult, op1=ALU.add).then_inc(qk_ready, 1)

            dve.wait_ge(qk_ready, 2 * TILES)
            dve.wait_ge(masks_ready, 3)

            def take_max(G, n):
                m = unit_no["A", G, n]
                qt, heads = a_unit(n)
                width = P * (qt + 1)
                dve.wait_ge(a_filled, m + 1)
                for e, hh in enumerate(heads):
                    taken = maxima_taken(G, n) - len(heads) + e
                    if taken >= 2:
                        dve.wait_ge(a_emptied, taken - 1)
                    nc.vector.tensor_tensor_reduce(
                        out=y[:, taken % 2, 0:width], in0=ps[:, m % 2, e * width:(e + 1) * width],
                        in1=mask[:, S - width:S], scale=1.0, scalar=MASKED, op0=ALU.add, op1=ALU.max,
                        accum_out=row_max[:, G % 2, qt, hh:hh + 1]).then_inc(a_emptied, 1)

            def shift(G):
                sq = stack_q[:, G % 3]
                m = row_max[:, G % 2]
                dve.wait_ge(a_emptied, maxima_taken(G, A_UNITS - 1))
                dve.wait_ge(t_filled, fill_no["QA", 1, G] + 1)
                link(nc.vector.tensor_copy(sq[:, :, :, 4], m))
                nc.vector.tensor_tensor(sq[:, :, :, 5], m, sq[:, :, :, 4].bitcast(F32),
                                        ALU.subtract).then_inc(shift_ready, 1)

            def evacuate_k(j, G):
                dve.wait_ge(t_filled, fill_no["K", j, G] + 1)
                if G < 4:
                    dve.wait_ge(k_zeroed, 2 * G + j + 1)
                nc.vector.tensor_copy(k_t[ROWS:P, G % 4, 2 * j + 1, :],
                                      ps[ROWS:P, fill_bank("K", j, G), :]).then_inc(t_emptied, 1)

            def normalise_output(G):
                g = G % GROUPS
                dve.wait_ge(o_turned, G + 1)
                turned = ps[:, PV, :].rearrange("p (t h d) -> p t h d", t=QT, h=GH)
                link(nc.vector.reciprocal(rsum[:, :, :], turned[:, :, :, HD]))
                dst = attn.rearrange("p t (h d) -> p t h d", d=HD)[:, :, GH * g:GH * g + GH, :]
                for qt in range(QT):
                    o = nc.vector.tensor_tensor(dst[:, qt], turned[:, qt, :, 0:HD],
                                                rsum[:, qt, :].unsqueeze(2).broadcast_to([P, GH, HD]), ALU.mult)
                o.then_inc(o_taken, 1)

            def attn_low(b, t):
                m = b * QT + t
                dve.wait_ge(at_hi_ready, m + 1)
                nc.vector.tensor_tensor(at_lo[:, m % 2], ps[:, TB, :].rearrange("p (k n) -> p k n", k=KC),
                                        at_hi[:, m % 2].bitcast(F32), ALU.subtract).then_inc(t_emptied, 1)

            def attn_added(b, t):
                u = unit_no["Y", b, t]
                dve.wait_ge(a_filled, u + 1)
                x_update(FFN_UPDATES + b * QT + t, projection_bank(b, t), 1.0)

            for s in STEPS:
                for i in range(B_OPS):
                    for n in (2 * i, 2 * i + 1):
                        if 0 <= s < NG and n < A_UNITS:
                            take_max(s, n)
                    for kind, j, G in fills_at(s, i):
                        if kind == "K":
                            evacuate_k(j, G)
                    if i == 0 and 0 <= s - 3 < NG:
                        normalise_output(s - 3)
                    if (s, i) == (NG, 0):
                        for t in range(3):
                            norm_stats(2, t)
                            norm_moments(2, t)
                            norm_apply(2, t)
                    if (s, i) in LOWS_AT:
                        turn_low(2, LOWS_AT[s, i])
                    if (s, i) == (NG, 5):
                        norm_stats(2, 3)
                        norm_moments(2, 3)
                        norm_apply(2, 3)
                if 0 <= s < NG:
                    shift(s)
                if s == 1:
                    dve.wait_ge(warmed, 1)
                    nc.vector.memset(ps[:, PV, :], 0.0).then_inc(pv_cleared, 1)
                    for p in WO_PIECES:
                        split_high(p)
                if s == OUTPROJ_STEP:
                    for t in range(QT + 1):
                        if t < QT:
                            attn_low(0, t)
                        if t >= 1:
                            attn_added(0, t - 1)

            normalise_output(NG - 1)
            attn_low(1, 0)
            gated(1, 0)
            for t in range(QT):
                if t + 1 < QT:
                    attn_low(1, t + 1)
                attn_added(1, t)
                norm_stats(2, QT + t)
                norm_moments(2, QT + t)
                norm_apply(2, QT + t)
            for t in range(QT, TILES):
                turn_low(2, t)
            ffn(1, 1)
            for t in range(TILES):
                out_tile(1, 1, t)

        @block.tensor
        def _(pe):
            def product(dst, w, v, first, last):
                nc.tensor.matmul(dst, w[0], v[0], start=first, stop=False)
                nc.tensor.matmul(dst, w[1], v[0], start=False, stop=False)
                return nc.tensor.matmul(dst, w[0], v[1], start=False, stop=last)

            def keep_warm(n, bank):
                for _ in range(n):
                    last = nc.tensor.matmul(ps[:, bank, :], ident_bf[:, :], mask[:, :], start=True, stop=True)
                return last

            def turn(phase, t):
                n = phase * TILES + t
                pe.wait_ge(norm_ready, n + 1)
                last_tile = n - (4 if phase == 0 else 2)
                if last_tile >= 0:
                    pe.wait_ge(xt_ready, last_tile + 1)
                for k in range(KC):
                    last = nc.tensor.transpose(ps[:, turn_bank(phase, t), k * P:(k + 1) * P],
                                               y[:, n % YS, k * P:(k + 1) * P], ident[:, :])
                last.then_inc(norm_turned, 1)

            def unit(f, u, between=None):
                c, b = UNIT_ORDER[u]
                n = UNITS * f + u
                pe.wait_ge(piece_lo, piece_no["gu", f, c] + 1)
                pe.wait_ge(xt_ready, 2 * TILES * f + 4 * (b + 1))
                if n >= 2:
                    pe.wait_ge(act_f_ready, n - 1)
                at = slice(512 * b, 512 * b + 512)
                for a, bank, done in ((0, n % 2, gate_done), (1, 2 + n % 2, up_done)):
                    for k in range(KC):
                        last = product(ps[:, bank, :], (gu_his[f][:, c % 2, a, k, :], gu_los[f][:, c % 2, a, k, :]),
                                       (xt_his[f][:, k, at], xt_los[f][:, k, at]), k == 0, k == KC - 1)
                        if k == KC - 1:
                            last.then_inc(done, 1)
                        if between and k % 2:
                            between(2 * a + k // 2)

            def down(f, r):
                chunks = range(FIRST * r, FIRST * r + FIRST)
                base = updates_before(f) + TILES * r
                pe.wait_ge(piece_lo, piece_no["wd", f, chunks[-2]] + 1)
                pe.wait_ge(act_ready, UNITS * f + 2 * chunks[-1])
                for t in range(TILES):
                    if t >= 2:
                        pe.wait_ge(x_updated, base + t - 1)
                    at = slice(t * P, (t + 1) * P)
                    for c in chunks:
                        if c == chunks[-1]:
                            pe.wait_ge(act_ready, UNITS * f + 2 * c + t // 4 + 1)
                            pe.wait_ge(piece_lo, piece_no["wd", f, c] + 1)
                        last = product(ps[:, 4 + t % 2, :], (act_his[f][:, slot_of(c), at], act_los[f][:, slot_of(c), at]),
                                       (wd_his[f][:, c % FIRST, :], wd_los[f][:, c % FIRST, :]),
                                       c == chunks[0], c == chunks[-1])
                    last.then_inc(down_done, 1)
                    if f == 0 and r == 1 and t >= AHEAD:
                        turn(1, t - AHEAD)

            def ffn(f, first):
                for u in range(first, UNITS):
                    if UNIT_ORDER[u] == (SLOTS, 0):
                        down(f, 0)
                    unit(f, u)
                down(f, 1)

            pe.wait_ge(ident_ready, 1)
            for t in range(4):
                turn(0, t)
            pe.wait_ge(masks_ready, 3)
            keep_warm(8, 3)
            unit(0, 0, between=lambda j: turn(0, 4 + j // 2) if j % 2 == 0 else None)
            unit(0, 1, between=lambda j: turn(0, 6 + j) if j < 2 else None)
            ffn(0, 2)
            for t in range(TILES):
                pe.wait_ge(xt_ready, TILES + t + 1)
                pe.wait_ge(piece_lo, piece_no[QK_PIECES[-1]] + 1)
                at = slice(t * P, (t + 1) * P)
                for j in range(3):
                    if t >= 2:
                        if j == 2:
                            pe.wait_ge(qkv_clipped, t - 1)
                        else:
                            pe.wait_ge(q_var_ready, 2 * (t - 2) + j + 1)
                    if j == 2:
                        pe.wait_ge(piece_lo, piece_no[V_PIECES[-1]] + 1)
                    hi, lo, cols = (v_hi, v_lo, slice(0, D)) if j == 2 else (qk_hi, qk_lo, slice(j * D, (j + 1) * D))
                    for k in range(KC):
                        last = product(ps[:, 3 * (t % 2) + j, :], (xt_hi[:, k, at], xt_lo[:, k, at]),
                                       (hi[:, k, cols], lo[:, k, cols]), k == 0, k == KC - 1)
                    last.then_inc(qkv_done, 1)
                    if t == 0 and j < AHEAD:
                        turn(1, TILES - AHEAD + j)

            def fill(kind, j, G):
                n = fill_no[kind, j, G]
                if kind == "QB":
                    pe.wait_ge(shift_ready, G + 1)
                else:
                    pe.wait_ge(stack_ready, G + 1)
                if n == 2:
                    pe.wait_ge(qkv_clipped, TILES - 1)
                elif n == 3:
                    pe.wait_ge(q_var_ready, 2 * (TILES - 1))
                elif n > 3:
                    pe.wait_ge(t_emptied, emptied_after[fill_at[n - 1]])
                bank = fill_bank(kind, j, G)
                for t in range(QT):
                    stack = stack_k[:, G % 2, t] if kind == "K" else stack_q[:, G % 3, t]
                    last = nc.tensor.matmul(ps[:, bank, t * P:(t + 1) * P],
                                            stack[:, 2 * j:2 * j + 2, :].rearrange("p h r -> p (h r)"),
                                            ident_r[:, :], start=True, stop=True)
                last.then_inc(t_filled, 1)

            def turn_output(G):
                pe.wait_ge(o_t_ready, G + 1)
                for t in range(QT):
                    last = nc.tensor.transpose(ps[:, PV, t * P:(t + 1) * P], o_t[:, t * P:(t + 1) * P], ident[:, :])
                last.then_inc(o_turned, 1)

            def unit_bank_free(m):
                if m >= 2:
                    kind, i, j = unit_at[m - 2]
                    if kind == "A":
                        pe.wait_ge(a_emptied, maxima_taken(i, j))
                    else:
                        pe.wait_ge(x_updated, FFN_UPDATES + QT * i + j + 1)

            def attn_turn(b, t):
                if t == 0:
                    pe.wait_ge(o_taken, GROUPS * (b + 1))
                pe.wait_ge(t_emptied, emptied_after[fill_at[fill_no["AT", b, t] - 1]])
                for k in range(KC):
                    last = nc.tensor.transpose(ps[:, TB, k * P:(k + 1) * P], attn[:, t, k * P:(k + 1) * P],
                                               ident[:, :])
                last.then_inc(t_filled, 1)

            def project(b, t):
                m, u = b * QT + t, unit_no["Y", b, t]
                pe.wait_ge(at_hi_ready, m + 1)
                pe.wait_ge(piece_lo, piece_no[WO_PIECES[1]] + 1)
                if b == 0 or t >= 2:
                    unit_bank_free(u)
                bank = projection_bank(b, t)
                for k in range(KC):
                    nc.tensor.matmul(ps[:, bank, :], at_hi[:, m % 2, k, :], wo_hi[:, k, :], start=k == 0, stop=False)
                    nc.tensor.matmul(ps[:, bank, :], at_hi[:, m % 2, k, :], wo_lo[:, k, :], start=False, stop=False)
                pe.wait_ge(t_emptied, emptied_after["AT", b, t])
                if t + 1 < QT:
                    attn_turn(b, t + 1)
                for k in range(KC):
                    last = nc.tensor.matmul(ps[:, bank, :], at_lo[:, m % 2, k, :], wo_hi[:, k, :], start=False,
                                            stop=k == KC - 1)
                last.then_inc(a_filled, 1)

            def pass_a(G, n):
                m = unit_no["A", G, n]
                qt, heads = a_unit(n)
                width = P * (qt + 1)
                if n in (0, 2):
                    pe.wait_ge(t_emptied, emptied_after["QA", n // 2, G])
                unit_bank_free(m)
                nc.tensor.matmul(ps[:, m % 2, 0:len(heads) * width].rearrange("p (h n) -> p h n", n=width),
                                 qa_t[:, G % 2, heads[0] // 2, qt * P:(qt + 1) * P],
                                 k_t[:, G % 4, heads[0]:heads[-1] + 1, 0:width],
                                 start=True, stop=True).then_inc(a_filled, 1)

            def pass_b(G, n):
                idx = B_OPS * G + n
                kc, heads = b_op(n)
                if n < 2:
                    pe.wait_ge(t_emptied, emptied_after["QB", n, G])
                if idx >= 2:
                    pe.wait_ge(exp_done, idx - 1)
                width = S - kc * P
                for hh, bank, col in heads:
                    nc.tensor.matmul(ps[:, 2 + 2 * (idx % 2) + bank, col:col + width],
                                     k_t[:, G % 4, hh, kc * P:(kc + 1) * P], qb_t[:, G % 2, hh // 2, kc * P:S],
                                     start=(col == 0), stop=False, skip_group_check=True)
                for hh, bank, col in heads:
                    last = nc.tensor.matmul(ps[:, 2 + 2 * (idx % 2) + bank, col:col + P], mask[:, S - P:S],
                                            ident_bf[:, :], start=False, stop=True, skip_group_check=True)
                last.then_inc(b_filled, 1)

            def probs_v(G, ops):
                b, g = G // GROUPS, G % GROUPS
                if 0 in ops:
                    pe.wait_ge(pv_cleared, 1)
                    if G >= 1:
                        pe.wait_ge(o_taken, G)
                pe.wait_ge(exp_done, B_OPS * G + ops[-1] + 1)
                for n in ops:
                    kc, heads = b_op(n)
                    width = S - kc * P
                    for e, (hh, _, _) in enumerate(heads):
                        last = nc.tensor.matmul(ps[32 * hh:32 * hh + VW, PV, kc * P:S],
                                                vext[:, b, kc, GH * g + hh, :],
                                                probs[:, (B_OPS * G + n) % 3, e * width:(e + 1) * width],
                                                start=(kc == 0), stop=(kc == QT - 1), skip_group_check=True,
                                                tile_position=(0, 32 * hh))
                last.then_inc(pv_step, len(ops))

            pe.wait_ge(vones_ready, 1)
            for s in STEPS:
                if s == -1:
                    pe.wait_ge(q_var_ready, 2 * (TILES - 1))
                elif s == 0:
                    pe.wait_ge(t_emptied, emptied_after["QA", 1, 0])
                elif s == 2:
                    pe.wait_ge(q_var_ready, 2 * TILES)
                    pe.wait_ge(qkv_clipped, TILES)
                for i in range(B_OPS):
                    if s < 2:
                        last = keep_warm(WARM, 0 if s < 0 else PV)
                        if (s, i) == (1, B_OPS - 1):
                            last.then_inc(warmed, 1)
                    if 0 <= s - 2 < NG:
                        pass_b(s - 2, i)
                    for n in (2 * i, 2 * i + 1):
                        if 0 <= s < NG and n < A_UNITS:
                            pass_a(s, n)
                    if i in PV_AT and 0 <= s - 2 < NG:
                        probs_v(s - 2, PV_AT[i])
                    if i == 0 and 0 <= s - 3 < NG:
                        turn_output(s - 3)
                    for kind, j, G in fills_at(s, i):
                        fill(kind, j, G)
                    if (s, i) in TURNS_AT:
                        turn(2, TURNS_AT[s, i])
                if 0 <= s - 2 < NG:
                    probs_v(s - 2, (B_OPS - 1,))
                if s == OUTPROJ_STEP:
                    attn_turn(0, 0)
                    for t in range(QT):
                        project(0, t)

            def last_attention(j):
                if j == 0:
                    turn_output(NG - 1)
                elif j == 2:
                    attn_turn(1, 0)

            unit(1, 0, between=last_attention)
            for t in range(QT):
                project(1, t)
            def last_turns(j):
                if j < 3:
                    turn(2, QT + j)
                if j == 2:
                    turn(2, TILES - 1)

            unit(1, 1, between=last_turns)
            ffn(1, 2)


def contraction_rows():
    slope = (1.0 / np.power(2.0, np.arange(1, H + 1) * (8.0 / H))).astype(np.float32)
    scale = np.exp2(np.floor(np.log2(slope)) - 11).astype(np.float32)
    hi = (np.round(slope / scale) * scale).astype(np.float32)
    lo = slope - hi
    pos = (np.arange(QT)[None, :] * P + np.arange(P)[:, None]).astype(np.float32)[:, :, None]
    rows_q = (hi, -pos, lo, -pos, 0.0, 0.0)
    rows_k = (pos, hi, pos, lo, -1.0, -1.0)
    return [np.ascontiguousarray(np.stack([np.broadcast_to(r, (P, QT, H)) for r in rows], -1), np.float32)
            for rows in (rows_q, rows_k)]


def kernel(L0_attn_hidden_states, L0_attn_w_qkv, L0_attn_q_ln_w, L0_attn_q_ln_b, L0_attn_k_ln_w, L0_attn_k_ln_b,
           L0_attn_w_out, L0_ffn_ln_w, L0_ffn_gate_w, L0_ffn_up_w, L0_ffn_down_w):
    import concourse.bacc as bacc
    from concourse.bass_utils import run_bass_kernel_spmd

    def turned(w, n):
        w = np.asarray(w)
        return w.reshape(w.shape[0] // n, n, KC, P).transpose(0, 3, 2, 1)

    w_gu = np.stack([turned(L0_ffn_gate_w, P), turned(L0_ffn_up_w, P)], 2)
    con_q, con_k = contraction_rows()
    arrays = {
        "x_in": np.asarray(L0_attn_hidden_states).reshape(B * S, D),
        "w_gu": w_gu.reshape(NCH, P, PIECE),
        "w_down": np.asarray(L0_ffn_down_w).T.reshape(NCH, P, D),
        "w_qkv": turned(L0_attn_w_qkv, 256).reshape(6, P, PIECE),
        "w_out": turned(L0_attn_w_out, 256).reshape(2, P, PIECE),
        "ln_w": np.asarray(L0_ffn_ln_w).reshape(1, D),
        "q_w": np.asarray(L0_attn_q_ln_w).reshape(1, D),
        "q_b": np.asarray(L0_attn_q_ln_b).reshape(1, D),
        "k_w": np.asarray(L0_attn_k_ln_w).reshape(1, D),
        "k_b": np.asarray(L0_attn_k_ln_b).reshape(1, D),
        "con_q": con_q,
        "con_k": con_k,
    }
    arrays = {name: np.ascontiguousarray(a) for name, a in arrays.items()}
    nc = bacc.Bacc("TRN2", target_bir_lowering=False, num_devices=1)
    ins = [nc.dram_tensor(name, a.shape, F32, kind="ExternalInput").ap() for name, a in arrays.items()]
    out = nc.dram_tensor("out", (B * S, D), F32, kind="ExternalOutput").ap()
    build(nc, *ins, out)
    got = run_bass_kernel_spmd(nc, [arrays], core_ids=[0])
    return got.results[0]["out"].reshape(B, S, D)
```
